# Optimizing a Trainium2 kernel written in Bass

```python
import numpy as np
import jax
import jax.numpy as jnp

def _softmax(x, axis=-1):
    return jax.nn.softmax(x, axis=axis)

def _gelu(x):
    return jax.nn.gelu(x, approximate=True)

def _silu(x):
    return jax.nn.silu(x)

def _sigmoid(x):
    return jax.nn.sigmoid(x)

def _layernorm(x, axis=-1, eps=1e-05):
    m = jnp.mean(x, axis=axis, keepdims=True)
    v = jnp.var(x, axis=axis, keepdims=True)
    return (x - m) / jnp.sqrt(v + eps)

def _scatter_add(tgt, idx, src, axis=0):
    return tgt.at[idx].add(src)

def _segment_sum(src, seg, n):
    return jax.ops.segment_sum(src, seg, n)
kernel_name = 'mk_adaln_ffn_d2_seqx_r8_5d6784'

def setup_inputs(seed: int=0):
    np.random.seed(seed)
    _w = jnp.asarray

    def _rec_inputs():
        import jax
        import jax.numpy as jnp
        _rk = jax.random.key(seed)
        x = -0.000125 + 0.9999 * jax.random.normal(jax.random.fold_in(_rk, 1), (128, 32, 512), jnp.float32)
        _lenS = 32 - jax.random.randint(jax.random.fold_in(_rk, 7), (128,), 0, max(1, 32 // 4) + 1, jnp.int32)
        _lenS2 = 32 - jax.random.randint(jax.random.fold_in(_rk, 8), (128,), 0, max(1, 32 // 4) + 1, jnp.int32)
        cond_128 = 0.0061147 + 1.02565 * jax.random.normal(jax.random.fold_in(_rk, 11), (128, 128), jnp.float32)
        fside_S_0 = -0.022604 + 0.987366 * jax.random.normal(jax.random.fold_in(_rk, 12), (32,), jnp.float32)
        return (x, cond_128, fside_S_0)
    x, cond_128, fside_S_0 = _rec_inputs()

    def _L0_cond_setup():
        import jax, jax.numpy as jnp
        import numpy as np
        K = 8
        T = 1.0
        D_EMBD = 128
        IN_C = 32
        OUT_C = 32
        BS = 32
        H = 512
        HID = 128
        key = jax.random.key(seed)
        ks = jax.random.split(key, 10)
        s = lambda fan_in: 1.0 / np.sqrt(fan_in)
        return {'x': jax.random.normal(ks[0], (BS, IN_C, H), dtype=jnp.float32), 'embedding': jax.random.normal(ks[1], (BS, D_EMBD), dtype=jnp.float32), 'W0': jax.random.normal(ks[2], (D_EMBD, HID), dtype=jnp.float32) * s(D_EMBD), 'b0': jnp.zeros((HID,), dtype=jnp.float32), 'W1': jax.random.normal(ks[3], (HID, HID), dtype=jnp.float32) * s(HID), 'b1': jnp.zeros((HID,), dtype=jnp.float32), 'W2': jax.random.normal(ks[4], (HID, K), dtype=jnp.float32) * s(HID), 'b2': jnp.zeros((K,), dtype=jnp.float32), 'weight': jax.random.normal(ks[5], (K, OUT_C, IN_C, 1), dtype=jnp.float32) * s(IN_C), 'bias_k': jax.random.normal(ks[6], (K, OUT_C), dtype=jnp.float32) * 0.1}
    _L0_cond_all = _L0_cond_setup()
    _L0_cond_in = {k: v for k, v in _L0_cond_all.items() if k in ('W0', 'b0', 'W1', 'b1', 'W2', 'b2', 'weight', 'bias_k')}
    del _L0_cond_all

    def _L0_ffn_setup():
        import jax, jax.numpy as jnp
        import numpy as np
        NUM_EXPERTS = 4
        HIDDEN = 512
        RANK = 8
        ALPHA = 8.0
        SCALE = ALPHA / RANK
        key = jax.random.key(seed)
        ks = jax.random.split(key, 6)
        B, T, H, E, R = (4, 512, HIDDEN, NUM_EXPERTS, RANK)
        x = jax.random.normal(ks[0], (B, T, H), dtype=jnp.float32)
        W_up = jax.random.normal(ks[1], (H, H), dtype=jnp.float32) / np.sqrt(H)
        gate_w = jax.random.normal(ks[2], (E, H), dtype=jnp.float32) / np.sqrt(H)
        expert_bias = jnp.zeros((E,), dtype=jnp.float32)
        lora_A = jax.random.normal(ks[3], (E, R, H), dtype=jnp.float32) / np.sqrt(H)
        lora_B = jax.random.normal(ks[4], (E, H, R), dtype=jnp.float32) * 0.01
        return {'x': x, 'W_up': W_up, 'gate_w': gate_w, 'expert_bias': expert_bias, 'lora_A': lora_A, 'lora_B': lora_B}
    _L0_ffn_all = _L0_ffn_setup()
    _L0_ffn_in = {k: v for k, v in _L0_ffn_all.items() if k in ('W_up', 'gate_w', 'expert_bias', 'lora_A', 'lora_B')}
    del _L0_ffn_all

    def _L1_cond_setup():
        import jax, jax.numpy as jnp
        import numpy as np
        from jax import lax
        N, C_IN, L = (32, 32, 512)
        C_OUT, K, GROUPS = (32, 9, 4)
        C_DIM, PAD, STRIDE = (128, 4, 1)
        key = jax.random.key(seed)
        k1, k2, k3, k4, k5 = jax.random.split(key, 5)
        x = jax.random.normal(k1, (N, C_IN, L), dtype=jnp.float32)
        c = jax.random.normal(k2, (N, C_DIM), dtype=jnp.float32)
        weight = jax.random.normal(k3, (C_OUT, C_IN // GROUPS, K), dtype=jnp.float32)
        c_weight = jax.random.normal(k4, (C_OUT, C_DIM), dtype=jnp.float32)
        bias = jax.random.normal(k5, (C_OUT,), dtype=jnp.float32)
        return {'x': x, 'c': c, 'weight': weight, 'c_weight': c_weight, 'bias': bias}
    _L1_cond_all = _L1_cond_setup()
    _L1_cond_in = {k: v for k, v in _L1_cond_all.items() if k in ('weight', 'c_weight')}
    del _L1_cond_all

    def _L1_ffn_setup():
        import jax, jax.numpy as jnp
        import numpy as np
        BATCH, TOK, DIM, OUT = (4, 256, 512, 512)
        E, R, TOP_K = (8, 16, 2)
        SCALING = 16.0 / R
        key = jax.random.key(seed)
        ks = jax.random.split(key, 6)
        return {'x': jax.random.normal(ks[0], (BATCH, TOK, DIM), dtype=jnp.float32), 'W_base': jax.random.normal(ks[1], (OUT, DIM), dtype=jnp.float32) / np.sqrt(DIM), 'b_base': jax.random.normal(ks[2], (OUT,), dtype=jnp.float32) * 0.01, 'W_gate': jax.random.normal(ks[3], (E, DIM), dtype=jnp.float32) * 0.01, 'A': jax.random.normal(ks[4], (E, R, DIM), dtype=jnp.float32) / np.sqrt(DIM), 'B': jax.random.normal(ks[5], (OUT, OUT // OUT * R * 0 + R), dtype=jnp.float32)[None].repeat(E, 0) * 0.0 + jax.random.normal(ks[5], (E, OUT, R), dtype=jnp.float32) * 0.02}
    _L1_ffn_all = _L1_ffn_setup()
    _L1_ffn_in = {k: v for k, v in _L1_ffn_all.items() if k in ('W_base', 'b_base', 'W_gate', 'A', 'B')}
    del _L1_ffn_all
    return {'x': x, 'cond_128': cond_128, 'fside_S_0': fside_S_0, 'L0_cond_W0': _L0_cond_in['W0'], 'L0_cond_b0': _L0_cond_in['b0'], 'L0_cond_W1': _L0_cond_in['W1'], 'L0_cond_b1': _L0_cond_in['b1'], 'L0_cond_W2': _L0_cond_in['W2'], 'L0_cond_b2': _L0_cond_in['b2'], 'L0_cond_weight': _L0_cond_in['weight'], 'L0_cond_bias_k': _L0_cond_in['bias_k'], 'L0_ffn_W_up': _L0_ffn_in['W_up'], 'L0_ffn_gate_w': _L0_ffn_in['gate_w'], 'L0_ffn_expert_bias': _L0_ffn_in['expert_bias'], 'L0_ffn_lora_A': _L0_ffn_in['lora_A'], 'L0_ffn_lora_B': _L0_ffn_in['lora_B'], 'L1_cond_weight': _L1_cond_in['weight'], 'L1_cond_c_weight': _L1_cond_in['c_weight'], 'L1_ffn_W_base': _L1_ffn_in['W_base'], 'L1_ffn_b_base': _L1_ffn_in['b_base'], 'L1_ffn_W_gate': _L1_ffn_in['W_gate'], 'L1_ffn_A': _L1_ffn_in['A'], 'L1_ffn_B': _L1_ffn_in['B']}

def reference(x, cond_128, fside_S_0, L0_cond_W0, L0_cond_b0, L0_cond_W1, L0_cond_b1, L0_cond_W2, L0_cond_b2, L0_cond_weight, L0_cond_bias_k, L0_ffn_W_up, L0_ffn_gate_w, L0_ffn_expert_bias, L0_ffn_lora_A, L0_ffn_lora_B, L1_cond_weight, L1_cond_c_weight, L1_ffn_W_base, L1_ffn_b_base, L1_ffn_W_gate, L1_ffn_A, L1_ffn_B):
    import jax
    import jax.numpy as jnp

    def _L0_cond_ref(x, embedding, W0, b0, W1, b1, W2, b2, weight, bias_k):
        import jax, jax.numpy as jnp
        import numpy as np
        K = 8
        T = 1.0
        D_EMBD = 128
        IN_C = 32
        OUT_C = 32
        BS = 32
        H = 512
        HID = 128
        h = jax.nn.gelu(embedding @ W0 + b0, approximate=False)
        h = jax.nn.gelu(h @ W1 + b1, approximate=False)
        att = jax.nn.softmax((h @ W2 + b2) / T, axis=-1)
        agg_w = jnp.einsum('bk,koi->boi', att, weight[..., 0])
        agg_b = att @ bias_k
        out = jnp.einsum('boi,bih->boh', agg_w, x) + agg_b[:, :, None]
        return out

    def _L0_ffn_ref(x, W_up, gate_w, expert_bias, lora_A, lora_B):
        import jax, jax.numpy as jnp
        import numpy as np
        NUM_EXPERTS = 4
        HIDDEN = 512
        RANK = 8
        ALPHA = 8.0
        SCALE = ALPHA / RANK
        B, T, H = x.shape
        E = gate_w.shape[0]
        x_flat = x.reshape(-1, H)
        logits = x_flat @ gate_w.T + expert_bias
        top1 = jnp.argmax(logits, axis=-1)
        one_hot = jax.nn.one_hot(top1, E, dtype=x_flat.dtype)
        base_out = jnp.einsum('bth,oh->bto', x, W_up)
        z = jnp.einsum('nh,erh->ner', x_flat, lora_A)
        d = jnp.einsum('ner,ehr->neh', z, lora_B) * SCALE
        delta = jnp.einsum('neh,ne->nh', d, one_hot)
        return base_out + delta.reshape(B, T, H)

    def _L1_cond_ref(x, c, weight, c_weight, bias):
        import jax, jax.numpy as jnp
        import numpy as np
        from jax import lax
        N, C_IN, L = (32, 32, 512)
        C_OUT, K, GROUPS = (32, 9, 4)
        C_DIM, PAD, STRIDE = (128, 4, 1)
        out = lax.conv_general_dilated(x, weight, window_strides=(STRIDE,), padding=[(PAD, PAD)], dimension_numbers=('NCH', 'OIH', 'NCH'), feature_group_count=GROUPS)
        ctx = jnp.einsum('nd,od->no', c, c_weight)
        out = out + ctx[:, :, None] + bias[None, :, None]
        return out

    def _L1_ffn_ref(x, W_base, b_base, W_gate, A, B):
        import jax, jax.numpy as jnp
        import numpy as np
        BATCH, TOK, DIM, OUT = (4, 256, 512, 512)
        E, R, TOP_K = (8, 16, 2)
        SCALING = 16.0 / R
        result = jnp.einsum('bnd,od->bno', x, W_base) + b_base
        logits = jnp.einsum('bnd,ed->bne', x, W_gate)
        probs = jax.nn.softmax(logits.astype(jnp.float32), axis=-1)
        top_p, top_i = jax.lax.top_k(probs, TOP_K)
        top_p = top_p / jnp.sum(top_p, axis=-1, keepdims=True)
        top_p = top_p.astype(x.dtype)
        route_w = jnp.sum(jax.nn.one_hot(top_i, E, dtype=x.dtype) * top_p[..., None], axis=-2)
        h = jnp.einsum('bnd,erd->bner', x, A)
        hw = h * route_w[..., None]
        delta = jnp.einsum('bner,eor->bno', hw, B)
        return result + delta * SCALING
    x = x + _L0_ffn_ref(_L0_cond_ref(x, cond_128, L0_cond_W0, L0_cond_b0, L0_cond_W1, L0_cond_b1, L0_cond_W2, L0_cond_b2, L0_cond_weight, L0_cond_bias_k), L0_ffn_W_up, L0_ffn_gate_w, L0_ffn_expert_bias, L0_ffn_lora_A, L0_ffn_lora_B)
    x = x + _L1_ffn_ref(_L1_cond_ref(x, cond_128, L1_cond_weight, L1_cond_c_weight, fside_S_0), L1_ffn_W_base, L1_ffn_b_base, L1_ffn_W_gate, L1_ffn_A, L1_ffn_B)
    return x

_drawn_inputs = setup_inputs


def setup_inputs(seed=0):
    import zlib

    import numpy as np

    out = dict(_drawn_inputs(seed))
    spreads = {'L0_cond_b0': (0.0, 0.8),
     'L0_cond_b1': (0.0, 0.514),
     'L0_cond_b2': (0.0, 0.492),
     'L0_ffn_expert_bias': (0.0, 0.8)}
    factors = {'L0_cond_bias_k': 2.887,
     'L0_ffn_gate_w': 8.0,
     'L0_ffn_lora_A': 8.0,
     'L0_ffn_lora_B': 8.0,
     'L1_ffn_b_base': 64.0}
    for name, (base, spread) in spreads.items():
        noise = np.random.default_rng([zlib.crc32(name.encode()), seed]).standard_normal(out[name].shape)
        drawn = base * np.exp(spread * noise) if base else spread * noise
        out[name] = jnp.asarray(drawn.astype(out[name].dtype))
    for name, factor in factors.items():
        out[name] = (out[name] * factor).astype(out[name].dtype)
    return out
```

```python
from contextlib import ExitStack

import concourse.bass as bass
from concourse import mybir

ALU = mybir.AluOpType
ACT = mybir.ActivationFunctionType
AX_X = mybir.AxisListType.X
F32 = mybir.dt.float32
F32R = mybir.dt.float32r
U32 = mybir.dt.uint32

P = 128
B = 128
C = 32
H = 512
SPT = P // C
NT = B // SPT
NQ = 4
NM = H // NQ
KC = H // P
E0, R0 = 4, 8
Z0 = E0 * R0
E1, R1 = 8, 16
KATT = 8
TAPS = 9
GROUPS = 4
GC = C // GROUPS
SLOTS = TAPS + NQ - 1
PAD = NM + 2
HALF = H // 2
L0W = H + Z0 + E0
L1W = HALF + E1 + P // 2
XQ = 16 * SPT
LOWEST = -3.4028234663852886e38


def adaln_ffn(nc, x, cond, fside, W0, b0, W1, b1, W2, b2, wmix, bias_k, w_up, gate_w,
              ebias, lora_a, lora_b, wconv, wctx, w_base, b_base, w_gate, a1, bb1, out):
    x_rows = x.rearrange("b c h -> (b c) h")
    out_rows = out.rearrange("b c h -> (b c) h")
    rows_dram = nc.dram_tensor("bias_rows", [2, B * C], F32, kind="Internal").ap()

    with ExitStack() as ctx:
        def sb(name, shape, dt=F32):
            return ctx.enter_context(nc.sbuf_tensor(name, shape, dt))

        def sem(name):
            return ctx.enter_context(nc.semaphore(name))

        def bank(name, banks=1):
            return ctx.enter_context(nc.psum_tensor(name, [P, banks, 512], F32))

        ps_mix, ps_conv, ps_z, ps_h = (bank(n) for n in ("ps_mix", "ps_conv", "ps_z", "ps_h"))
        ps_up, ps_base = bank("ps_up", 2), bank("ps_base", 2)

        cond_s, W0_s, W1_s = sb("cond_s", [P, P]), sb("W0_s", [P, P]), sb("W1_s", [P, P])
        W2_s, b0_s, b1_s = sb("W2_s", [P, KATT]), sb("b0_s", [P, 1]), sb("b1_s", [P, 1])
        b2_s, fside_s = sb("b2_s", [P, KATT]), sb("fside_s", [P, C])
        biask_s, wctx_s = sb("biask_s", [KATT, C]), sb("wctx_s", [C, P])
        wmix_s, wconv_s = sb("wmix_s", [C, KATT, C]), sb("wconv_s", [C, GC * TAPS])
        ebias_s, bbase_s = sb("ebias_s", [P, E0]), sb("bbase_s", [P, H])
        wup_raw, wbase_raw = sb("wup_raw", [P, NQ, H]), sb("wbase_raw", [P, KC, H])
        ga_raw, a1_raw, g1_raw = sb("ga_raw", [Z0 + E0, H]), sb("a1_raw", [P, H]), sb("g1_raw", [E1, H])
        lb_raw, b1m_raw = sb("lb_raw", [P, E0, NQ, R0]), sb("b1m_raw", [P, E1, NQ, R1])

        ident = sb("ident", [P, P])
        ones = sb("ones", [P, P])
        quad = sb("quad", [P, SPT])
        lane4 = sb("lane4", [P, SPT])
        tile_of = sb("tile_of", [P, NT])
        group_of = sb("group_of", [C, GROUPS])
        iota8, iota_e = sb("iota8", [P, E1]), sb("iota_e", [P, E0, R0])

        condT, wctxT = sb("condT", [P, P]), sb("wctxT", [P, C])
        h1T, h2T = sb("h1T", [P, P]), sb("h2T", [P, P])
        lg, mx, negm = sb("lg", [P, KATT]), sb("mx", [P, 1]), sb("negm", [P, 1])
        ex, exsum, exrec = sb("ex", [P, KATT]), sb("exsum", [P, 1]), sb("exrec", [P, 1])
        att, attT = sb("att", [P, KATT]), sb("attT", [KATT, P])
        att_spread = sb("att_spread", [P, NT, KATT])
        comb = sb("comb", [P, 2, C])
        att_b = sb("att_b", [P, NT, KATT])
        wmix_t = sb("wmix_t", [P, C, KATT])
        rows = sb("rows", [P, 2, B * C])

        up_hi, up_lo = sb("up_hi", [P, KC, L0W], F32R), sb("up_lo", [P, KC, L0W], F32R)
        base_hi = sb("base_hi", [P, NQ, 2, L1W], F32R)
        base_lo = sb("base_lo", [P, NQ, 2, L1W], F32R)
        lb_w, lb_tmp = sb("lb_w", [3 * Z0, H], F32R), sb("lb_tmp", [3 * Z0, H], F32R)
        b1_hi, b1_lo = sb("b1_hi", [P, H], F32R), sb("b1_lo", [P, H], F32R)
        taps = sb("taps", [C, GROUPS, GC, TAPS + 2 * (NQ - 1)])
        taps_q = sb("taps_q", [C, SLOTS, C, NQ])
        conv_w = sb("conv_w", [P, SLOTS, C])

        wmix_rep = sb("wmix_rep", [C, KATT, SPT, C])
        lane_rep = sb("lane_rep", [P, SPT, C])
        lb_rep = sb("lb_rep", [P, NQ, 3, E0, R0])
        b1m_t = sb("b1m_t", [P, NQ, E1, R1])

        xt = sb("xt", [P, 2, H])
        prod, gsum = sb("prod", [P, C, KATT]), sb("gsum", [P, C])
        mix_w = sb("mix_w", [P, SPT, C])
        y32, y_hi, y_lo = sb("y32", [P, KC, P]), sb("y_hi", [P, KC, P], F32R), sb("y_lo", [P, KC, P], F32R)
        gl0, m80, ix0 = sb("gl0", [P, 8]), sb("m80", [P, 8]), sb("ix0", [P, 8], U32)
        ixf0, zm, zc = sb("ixf0", [P, 1]), sb("zm", [P, E0, R0]), sb("zc", [P, 3, Z0], F32R)
        zT = sb("zT", [3 * Z0, P], F32R)
        x1p = sb("x1p", [P, NQ, NM])
        x1b = sb("x1b", [P, 2, H])
        xq = sb("xq", [P, SPT, PAD])
        c32, c_hi, c_lo = sb("c32", [P, NQ, P]), sb("c_hi", [P, NQ, P], F32R), sb("c_lo", [P, NQ, P], F32R)
        m81, ix1, ixf1 = sb("m81", [P, 8]), sb("ix1", [P, 8], U32), sb("ixf1", [P, 2])
        d2, e2, esum, erec = sb("d2", [P, 2]), sb("e2", [P, 2]), sb("esum", [P, 1]), sb("erec", [P, 1])
        r0, r1, route = sb("r0", [P, E1]), sb("r1", [P, E1]), sb("route", [P, E1])
        hw = sb("hw", [P, E1, R1])
        hT_hi, hT_lo = sb("hT_hi", [P, P], F32R), sb("hT_lo", [P, P], F32R)
        ot = sb("ot", [P, 2, H])

        in_cond, in_mix, in_conv = sem("in_cond"), sem("in_mix"), sem("in_conv")
        in_up, in_small0, in_base, in_small1 = sem("in_up"), sem("in_small0"), sem("in_base"), sem("in_small1")
        x_in = [sem("x_in0"), sem("x_in1")]
        rows_out, rows_in = sem("rows_out"), sem("rows_in")
        xq_in, stored = sem("xq_in"), [sem("stored0"), sem("stored1")]
        ident_zero, ident_ready, consts_ready = sem("ident_zero"), sem("ident_ready"), sem("consts_ready")
        masks_ready, taps_zero, taps_ready = sem("masks_ready"), sem("taps_zero"), sem("taps_ready")
        cond_turned, cond_copied = sem("cond_turned"), sem("cond_copied")
        ctx_done, ctx_copied = sem("ctx_done"), sem("ctx_copied")
        mlp_done, gelu_done = sem("mlp_done"), sem("gelu_done")
        att_step, exp_done, att_turned = sem("att_step"), sem("exp_done"), sem("att_turned")
        attT_copied, spread_ready, aggb_done, attb_done = (sem("attT_copied"), sem("spread_ready"),
                                                           sem("aggb_done"), sem("attb_done"))
        comb_ready, attb_ready = sem("comb_ready"), sem("attb_ready")
        wmix_turned, wmix_ready, conv_turned, conv_ready = (sem("wmix_turned"), sem("wmix_ready"),
                                                            sem("conv_turned"), sem("conv_ready"))
        wmix_copied, lane_copied, lb_copied, b1_copied = (sem("wmix_copied"), sem("lane_copied"),
                                                          sem("lb_copied"), sem("b1_copied"))
        fill_done, fill_hi, fill_lo = sem("fill_done"), sem("fill_hi"), sem("fill_lo")
        prod_done, gsum_done, mixw_done = sem("prod_done"), sem("gsum_done"), sem("mixw_done")
        mix_done, y32_done, yhi_done, ylo_done = sem("mix_done"), sem("y32_done"), sem("yhi_done"), sem("ylo_done")
        up_done, gate0_step, z_ready, zt_done, zT_ready = (sem("up_done"), sem("gate0_step"), sem("z_ready"),
                                                           sem("zt_done"), sem("zT_ready"))
        lb_done, x1_done, x1b_done = sem("lb_done"), sem("x1_done"), sem("x1b_done")
        conv_done, c32_done, chi_done, clo_done = sem("conv_done"), sem("c32_done"), sem("chi_done"), sem("clo_done")
        base_done, gate1_step, d2_ready, e2_ready, hw_done = (sem("base_done"), sem("gate1_step"), sem("d2_ready"),
                                                              sem("e2_ready"), sem("hw_done"))
        ht_done, hthi_done, htlo_done = sem("ht_done"), sem("hthi_done"), sem("htlo_done")
        delta_done, out_done = sem("delta_done"), sem("out_done")

        FILL_BANKS = [ps_up[:, 0], ps_up[:, 1], ps_base[:, 0], ps_base[:, 1]]
        fills = []
        for q in range(NQ):
            cols = slice(q * NM, (q + 1) * NM)
            fills.append(((in_up, 16), [wup_raw[:, q, k * P:(k + 1) * P] for k in range(KC)], KC, NM,
                          up_hi[:, :, cols], up_lo[:, :, cols]))
        ga = [ga_raw[:, k * P:(k + 1) * P] for k in range(KC)]
        fills.append(((in_small0, 48), ga, KC, Z0 + E0, up_hi[:, :, H:L0W], up_lo[:, :, H:L0W]))
        LB_FILL = len(fills)
        fills.append(((lb_copied, 1), [lb_rep[:, q].rearrange("m a e r -> m (a e r)")
                                        for q in range(NQ)], NQ, NM, None, None))
        for q in range(NQ):
            fills.append(((in_base, 16), [wbase_raw[:, dc, q:H:NQ] for dc in range(KC)], KC, P,
                          base_hi[:, q, :, 0:HALF].rearrange("m j (k d) -> m j k d", k=2),
                          base_lo[:, q, :, 0:HALF].rearrange("m j (k d) -> m j k d", k=2)))
        fills.append(((in_small1, 48), [g1_raw[:, q:H:NQ] for q in range(NQ)], NQ, E1,
                      base_hi[:, :, 0, HALF:HALF + E1], base_lo[:, :, 0, HALF:HALF + E1]))
        fills.append(((in_small1, 48), [a1_raw[:, q:H:NQ] for q in range(NQ)], NQ, P,
                      base_hi[:, :, :, HALF + E1:L1W], base_lo[:, :, :, HALF + E1:L1W]))
        fills.append(((b1_copied, 1), [b1m_t[:, q].rearrange("m e r -> m (e r)") for q in range(NQ)], NQ, NM,
                      b1_hi[:].rearrange("p (m q) -> p q m", q=NQ), b1_lo[:].rearrange("p (m q) -> p q m", q=NQ)))
        NF = len(fills)
        NF0 = LB_FILL + 1

        def fill_bank(n, parts=P):
            _, _, cnt, width, hi, _ = fills[n]
            v = FILL_BANKS[n % 4][0:parts, 0:cnt * width].rearrange("p (k d) -> p k d", k=cnt)
            if hi is not None and len(hi.shape) == 4:
                if hi.shape[2] == 2 and hi.shape[1] == 2:
                    v = v.rearrange("p (j k) d -> p j k d", j=2)
                else:
                    v = v.rearrange("p k (j d) -> p k j d", j=2)
            return v

        def once(tile):
            return not isinstance(tile, int) or 0 <= tile < NT

        def after(eng, sem, count):
            if not isinstance(count, int) or count > 0:
                eng.wait_ge(sem, count)

        FIRST, LAST = 4, NT - 2
        STEPS = NT + 2

        def iterate(eng, body):
            for i in range(FIRST):
                body(i, i % 2)
            with eng.Fori(FIRST // 2, LAST // 2) as pair:
                body(pair * 2, 0)
                body(pair * 2 + 1, 1)
            for i in range(LAST, STEPS):
                body(i, i % 2)

        def pair_count(i, par, off):
            return (i + (off - (par + off) % 2)) * 8 + 16

        block = ctx.enter_context(nc.Block())

        @block.sync
        def _(sp):
            def load_x(t, par):
                sp.dma_start(xt[:, par], x_rows[bass.ds(t * P, P), :]).then_inc(x_in[par], 16)

            sp.dma_start(cond_s[:], cond).then_inc(in_cond, 16)
            sp.dma_start(wctx_s[:], wctx).then_inc(in_cond, 16)
            sp.dma_start(W0_s[:], W0).then_inc(in_cond, 16)
            sp.dma_start(b0_s[:], b0.rearrange("(p a) -> p a", a=1)).then_inc(in_cond, 16)
            sp.dma_start(W1_s[:], W1).then_inc(in_cond, 16)
            sp.dma_start(b1_s[:], b1.rearrange("(p a) -> p a", a=1)).then_inc(in_cond, 16)
            sp.dma_start(W2_s[:], W2).then_inc(in_cond, 16)
            sp.dma_start(biask_s[:], bias_k).then_inc(in_cond, 16)
            sp.dma_start(b2_s[:], b2.partition_broadcast(P)).then_inc(in_cond, 16)
            sp.dma_start(fside_s[:], fside.partition_broadcast(P)).then_inc(in_cond, 16)
            sp.dma_start(wmix_s[:], wmix.rearrange("k o i a -> o k (i a)")).then_inc(in_mix, 16)
            load_x(0, 0)
            load_x(1, 1)
            sp.dma_start(wbase_raw[:], w_base.rearrange("(k p) h -> p k h", p=P)).then_inc(in_base, 16)
            sp.dma_start(a1_raw[:], a1.rearrange("e r d -> (e r) d")).then_inc(in_small1, 16)
            sp.dma_start(g1_raw[:], w_gate).then_inc(in_small1, 16)
            sp.dma_start(b1m_raw[:].rearrange("m e q r -> m e (q r)"), bb1.rearrange("e (m q) r -> m e (q r)", q=NQ)).then_inc(in_small1, 16)
            sp.wait_ge(comb_ready, 2)
            for j in range(2):
                sp.dma_start(rows_dram[j].rearrange("(b o) -> b o", b=B), comb[:, j]).then_inc(rows_out, 16)
            sp.wait_ge(rows_out, 32)
            for j in range(2):
                sp.dma_start(rows[:, j], rows_dram[j].partition_broadcast(P)).then_inc(rows_in, 16)

            def body(i, par):
                if once(i):
                    sp.wait_ge(x1_done, i + 1)
                    for b in range(SPT):
                        sp.dma_start(xq[:, b, 1:1 + NM], x1p[b * C:(b + 1) * C]).then_inc(xq_in, 16)
                    if not isinstance(i, int) or i + 2 < NT:
                        load_x(i + 2, par)
                if once(i - 2):
                    sp.wait_ge(out_done, i - 1)
                    sp.dma_start(out_rows[bass.ds((i - 2) * P, P), :], ot[:, par]).then_inc(stored[par], 16)

            iterate(sp, body)
            for par in range(2):
                sp.wait_ge(stored[par], 16 * (NT // 2))

        @block.gpsimd
        def _(pool):
            pool.memset(ident[:], 0.0).then_inc(ident_zero, 1)
            pool.wait_ge(ident_zero, 1)
            pool.affine_select(out=ident[:], in_=ident[:], compare_op=ALU.not_equal, fill=1.0, base=0,
                               pattern=[[-1, P]], channel_multiplier=1).then_inc(ident_ready, 1)
            pool.iota(iota8[:], [[1, E1]], base=0, channel_multiplier=0,
                      allow_small_or_imprecise_dtypes=True).then_inc(consts_ready, 1)
            pool.iota(iota_e[:], [[1, E0], [0, R0]], base=0, channel_multiplier=0,
                      allow_small_or_imprecise_dtypes=True).then_inc(consts_ready, 1)
            pool.memset(base_hi[:, :, 1, HALF:HALF + E1].bitcast(F32), 0.0).then_inc(consts_ready, 1)
            pool.memset(base_lo[:, :, 1, HALF:HALF + E1].bitcast(F32), 0.0).then_inc(consts_ready, 1)
            pool.memset(xq[:], 0.0).then_inc(consts_ready, 1)

            def make_prod(t):
                after(pool, gsum_done, t)
                pool.tensor_tensor(prod[:], wmix_t[:], att_b[:, bass.ds(t, 1), :].to_broadcast([P, C, KATT]),
                                   ALU.mult).then_inc(prod_done, 1)

            pool.wait_ge(in_mix, 16)
            pool.tensor_copy(wmix_rep[:], wmix_s[:].unsqueeze(2).to_broadcast([C, KATT, SPT, C]))\
                .then_inc(wmix_copied, 1)
            pool.wait_ge(masks_ready, 6)
            pool.tensor_copy(lane_rep[:], lane4[:].unsqueeze(2).to_broadcast([P, SPT, C])).then_inc(lane_copied, 1)
            pool.wait_ge(in_small0, 48)
            for n in range(3):
                cp = pool.tensor_copy(lb_rep[:, :, n], lb_raw[:].rearrange("m e q r -> m q e r"))
            cp.then_inc(lb_copied, 1)
            pool.wait_ge(in_small1, 48)
            pool.tensor_copy(b1m_t[:], b1m_raw[:].rearrange("m e q r -> m q e r")).then_inc(b1_copied, 1)
            pool.wait_ge(attb_ready, 1)
            pool.wait_ge(wmix_ready, 1)
            make_prod(0)
            make_prod(1)
            pool.wait_ge(y32_done, 1)
            pool.wait_ge(yhi_done, 1)
            pool.tensor_tensor(y_lo[:], y32[:], y_hi[:], ALU.subtract).then_inc(ylo_done, 1)

            def body(i, par):
                if once(i + 2):
                    make_prod(i + 2)
                if once(i - 1):
                    pool.wait_ge(c32_done, i)
                    pool.wait_ge(chi_done, i)
                    pool.tensor_tensor(c_lo[:], c32[:], c_hi[:], ALU.subtract).then_inc(clo_done, 1)
                if once(i + 1):
                    pool.wait_ge(y32_done, i + 2)
                    pool.wait_ge(yhi_done, i + 2)
                    pool.tensor_tensor(y_lo[:], y32[:], y_hi[:], ALU.subtract).then_inc(ylo_done, 1)
                if once(i):
                    pool.wait_ge(x1_done, i + 1)
                    after(pool, out_done, i - 1)
                    pool.tensor_tensor(x1b[:, par].rearrange("p (m q) -> p m q", q=NQ),
                                       x1p[:].rearrange("p q m -> p m q"),
                                       bbase_s[:].rearrange("p (m q) -> p m q", q=NQ),
                                       ALU.add).then_inc(x1b_done, 1)

            iterate(pool, body)

        @block.scalar
        def _(act):
            act.dma_start(wup_raw[:], w_up.rearrange("(m q) h -> m q h", q=NQ)).then_inc(in_up, 16)
            act.dma_start(ga_raw[0:Z0], lora_a.rearrange("e r h -> (e r) h")).then_inc(in_small0, 16)
            act.dma_start(ga_raw[Z0:Z0 + E0], gate_w).then_inc(in_small0, 16)
            act.dma_start(lb_raw[:].rearrange("m e q r -> m e (q r)"), lora_b.rearrange("e (m q) r -> m e (q r)", q=NQ)).then_inc(in_small0, 16)
            act.dma_start(wconv_s[:], wconv.rearrange("o i k -> o (i k)")).then_inc(in_conv, 16)
            act.dma_start(ebias_s[:], ebias.partition_broadcast(P)).then_inc(in_conv, 16)
            act.dma_start(bbase_s[:], b_base.partition_broadcast(P)).then_inc(in_conv, 16)
            act.wait_ge(in_cond, 160)
            act.wait_ge(mlp_done, 1)
            act.activation(h1T[:], ps_mix[:, 0, 0:P], ACT.Gelu, bias=b0_s[:, 0:1]).then_inc(gelu_done, 1)
            act.wait_ge(mlp_done, 2)
            act.activation(h2T[:], ps_mix[:, 0, 0:P], ACT.Gelu, bias=b1_s[:, 0:1]).then_inc(gelu_done, 1)
            act.wait_ge(att_step, 3)
            act.activation(ex[:], lg[:], ACT.Exp, bias=negm[:, 0:1], accum_out=exsum[:, 0:1]).then_inc(exp_done, 1)

            def high_part(n):
                act.wait_ge(fill_done, n + 1)
                if n == LB_FILL:
                    v = fill_bank(n, 3 * Z0)
                    act.activation(lb_w[0:2 * Z0].rearrange("p (k d) -> p k d", k=NQ), v[0:2 * Z0],
                                   ACT.Copy).then_inc(fill_hi, 1)
                    act.activation(lb_tmp[2 * Z0:].rearrange("p (k d) -> p k d", k=NQ), v[2 * Z0:],
                                   ACT.Copy).then_inc(fill_hi, 1)
                else:
                    act.activation(fills[n][4], fill_bank(n), ACT.Copy).then_inc(fill_hi, 1)

            def y_high(t):
                act.wait_ge(y32_done, t + 1)
                act.activation(y_hi[:], y32[:], ACT.Copy).then_inc(yhi_done, 1)

            for n in range(NF):
                high_part(n)
            y_high(0)

            def body(i, par):
                if once(i - 2):
                    act.wait_ge(d2_ready, i - 1)
                    act.activation(e2[:], d2[:], ACT.Exp, accum_out=esum[:, 0:1]).then_inc(e2_ready, 1)
                    act.wait_ge(ht_done, i - 1)
                    act.activation(hT_hi[:], ps_h[:, 0, 0:P], ACT.Copy).then_inc(hthi_done, 1)
                if once(i):
                    act.wait_ge(zt_done, i + 1)
                    act.activation(zT[:], ps_z[0:3 * Z0, 0, 0:P], ACT.Copy).then_inc(zT_ready, 1)
                if once(i - 1):
                    act.wait_ge(c32_done, i)
                    act.activation(c_hi[:], c32[:], ACT.Copy).then_inc(chi_done, 1)
                if once(i + 1):
                    y_high(i + 1)

            iterate(act, body)

        @block.vector
        def _(dve):
            dve.wait_ge(ident_ready, 1)
            dve.memset(ones[:], 1.0).then_inc(masks_ready, 1)
            dve.tensor_reduce(quad[:], ident[:].rearrange("p (j r) -> p j r", j=SPT), AX_X, ALU.add)\
                .then_inc(masks_ready, 1)
            dve.tensor_reduce(lane4[:], ident[:].rearrange("p (t j) -> p j t", j=SPT), AX_X, ALU.add)\
                .then_inc(masks_ready, 1)
            dve.tensor_reduce(tile_of[:], ident[:].rearrange("p (t j) -> p t j", j=SPT), AX_X, ALU.add)\
                .then_inc(masks_ready, 1)
            dve.tensor_reduce(group_of[:], ident[0:C, 0:C].rearrange("p (g r) -> p g r", g=GROUPS), AX_X, ALU.add)\
                .then_inc(masks_ready, 1)
            dve.memset(gl0[:], LOWEST).then_inc(masks_ready, 1)
            dve.memset(taps[:], 0.0).then_inc(taps_zero, 1)

            dve.wait_ge(cond_turned, 1)
            dve.tensor_copy(condT[:], ps_mix[:, 0, 0:P]).then_inc(cond_copied, 1)
            dve.wait_ge(cond_turned, 2)
            dve.tensor_copy(wctxT[:], ps_conv[:, 0, 0:C]).then_inc(cond_copied, 1)
            dve.wait_ge(in_conv, 48)
            dve.wait_ge(taps_zero, 1)
            dve.wait_ge(masks_ready, 6)
            dve.tensor_tensor(taps[:, :, :, NQ - 1:NQ - 1 + TAPS],
                              wconv_s[:].rearrange("o (i k) -> o i k", k=TAPS).unsqueeze(1)
                              .to_broadcast([C, GROUPS, GC, TAPS]),
                              group_of[:].unsqueeze(2).unsqueeze(3).to_broadcast([C, GROUPS, GC, TAPS]),
                              ALU.mult).then_inc(taps_ready, 1)
            dve.wait_ge(taps_ready, 1)
            for q in range(NQ):
                dve.tensor_copy(taps_q[:, :, :, q],
                                taps[:, :, :, q:q + SLOTS].rearrange("o g i s -> o s (g i)"))\
                    .then_inc(taps_ready, 1)
            dve.wait_ge(ctx_done, 1)
            dve.wait_ge(in_cond, 160)
            dve.tensor_tensor(comb[:, 1], ps_conv[:, 0, 0:C], fside_s[:], ALU.add).then_inc(comb_ready, 1)
            dve.wait_ge(mlp_done, 3)
            dve.tensor_tensor(lg[:], ps_mix[:, 0, 0:KATT], b2_s[:], ALU.add).then_inc(att_step, 1)
            dve.wait_ge(att_step, 1)
            dve.reduce_max(mx[:], lg[:], AX_X).then_inc(att_step, 1)
            dve.wait_ge(att_step, 2)
            dve.tensor_scalar(negm[:], mx[:], -1.0, None, ALU.mult).then_inc(att_step, 1)
            dve.wait_ge(exp_done, 1)
            dve.reciprocal(exrec[:], exsum[:]).then_inc(att_step, 1)
            dve.wait_ge(att_step, 4)
            dve.tensor_scalar(att[:], ex[:], exrec[:, 0:1], None, ALU.mult).then_inc(att_step, 1)
            dve.wait_ge(att_step, 5)
            dve.tensor_tensor(att_spread[:], tile_of[:].unsqueeze(2).to_broadcast([P, NT, KATT]),
                              att[:].unsqueeze(1).to_broadcast([P, NT, KATT]), ALU.mult)\
                .then_inc(spread_ready, 1)
            dve.wait_ge(att_turned, 1)
            dve.tensor_copy(attT[:], ps_mix[0:KATT, 0, 0:P]).then_inc(attT_copied, 1)
            dve.wait_ge(wmix_turned, 1)
            dve.tensor_copy(wmix_t[:], ps_h[:, 0, 0:KATT * C].rearrange("p (k o) -> p o k", k=KATT))\
                .then_inc(wmix_ready, 1)
            dve.wait_ge(aggb_done, 1)
            dve.tensor_copy(comb[:, 0], ps_mix[:, 0, 0:C]).then_inc(comb_ready, 1)
            dve.wait_ge(attb_done, 1)
            dve.tensor_copy(att_b[:], ps_conv[:, 0, 0:NT * KATT].rearrange("p (t k) -> p t k", k=KATT))\
                .then_inc(attb_ready, 1)
            dve.wait_ge(conv_turned, 1)
            dve.tensor_copy(conv_w[:], ps_z[:, 0, 0:SLOTS * C].rearrange("p (s o) -> p s o", s=SLOTS))\
                .then_inc(conv_ready, 1)

            def low_part(n):
                dve.wait_ge(fill_hi, n + 1 + (n >= LB_FILL))
                if n == LB_FILL:
                    dve.tensor_tensor(lb_w[2 * Z0:].rearrange("p (k d) -> p k d", k=NQ),
                                      fill_bank(n, 3 * Z0)[2 * Z0:],
                                      lb_tmp[2 * Z0:].rearrange("p (k d) -> p k d", k=NQ),
                                      ALU.subtract).then_inc(fill_lo, 1)
                else:
                    dve.tensor_tensor(fills[n][5], fill_bank(n), fills[n][4], ALU.subtract).then_inc(fill_lo, 1)

            def mix_sums(t):
                dve.wait_ge(prod_done, t + 1)
                dve.tensor_reduce(gsum[:], prod[:], AX_X, ALU.add).then_inc(gsum_done, 1)

            def mix_blocks(t):
                dve.wait_ge(gsum_done, t + 1)
                after(dve, mix_done, t)
                dve.tensor_tensor(mix_w[:], gsum[:].unsqueeze(1).to_broadcast([P, SPT, C]),
                                  quad[:].unsqueeze(2).to_broadcast([P, SPT, C]), ALU.mult)\
                    .then_inc(mixw_done, 1)

            def y_sum(t):
                dve.wait_ge(mix_done, t + 1)
                after(dve, ylo_done, t)
                dve.tensor_tensor(y32[:], ps_mix[:, 0].rearrange("p (k r) -> p k r", k=KC),
                                  rows[:, 0, bass.ds(t * P, P)].unsqueeze(1).to_broadcast([P, KC, P]),
                                  ALU.add).then_inc(y32_done, 1)

            mix_sums(0)
            mix_blocks(0)
            for n in range(NF):
                low_part(n)
            dve.wait_ge(rows_in, 32)
            y_sum(0)

            def turned_low(t):
                dve.wait_ge(hthi_done, t + 1)
                dve.tensor_tensor(hT_lo[:], ps_h[:, 0, 0:P], hT_hi[:], ALU.subtract).then_inc(htlo_done, 1)

            G1 = 6
            G0 = 4

            def body(i, par):
                if once(i - 2):
                    t = i - 2
                    logits = ps_base[:, 0, HALF:HALF + E1]
                    dve.wait_ge(base_done, t + 1)
                    if once(i + 1):
                        mix_sums(i + 1)
                    dve.max(m81[:], logits).then_inc(gate1_step, 1)
                    dve.wait_ge(gate1_step, t * G1 + 1)
                    dve.tensor_scalar(d2[:], m81[:, 0:2], m81[:, 0:1], None, ALU.subtract).then_inc(d2_ready, 1)
                    dve.max_index(ix1[:], m81[:], logits).then_inc(gate1_step, 1)
                    dve.wait_ge(gate1_step, t * G1 + 2)
                    dve.tensor_copy(ixf1[:], ix1[:, 0:2]).then_inc(gate1_step, 1)
                    dve.wait_ge(e2_ready, t + 1)
                    dve.reciprocal(erec[:], esum[:]).then_inc(gate1_step, 1)
                    dve.wait_ge(gate1_step, t * G1 + 3)
                    dve.tensor_scalar(r0[:], iota8[:], ixf1[:, 0:1], e2[:, 0:1], ALU.is_equal, ALU.mult)
                    dve.tensor_scalar(r1[:], iota8[:], ixf1[:, 1:2], e2[:, 1:2], ALU.is_equal, ALU.mult)\
                        .then_inc(gate1_step, 1)
                    dve.wait_ge(gate1_step, t * G1 + 5)
                    dve.tensor_tensor(route[:], r0[:], r1[:], ALU.add).then_inc(gate1_step, 1)
                    dve.wait_ge(gate1_step, t * G1 + 6)
                    after(dve, ht_done, t)
                    for j in range(2):
                        e = slice(j * E1 // 2, (j + 1) * E1 // 2)
                        dve.scalar_tensor_tensor(
                            hw[:, e], ps_base[:, j, HALF + E1:L1W].rearrange("p (e r) -> p e r", r=R1),
                            erec[:, 0:1], route[:, e].unsqueeze(2).to_broadcast([P, E1 // 2, R1]),
                            ALU.mult, ALU.mult).then_inc(hw_done, 1)
                elif once(i + 1):
                    mix_sums(i + 1)
                if once(i):
                    dve.wait_ge(up_done, i + 1)
                    dve.tensor_tensor(gl0[:, 0:E0], ps_up[:, 1, HALF + Z0:HALF + Z0 + E0], ebias_s[:], ALU.add)\
                        .then_inc(gate0_step, 1)
                    dve.wait_ge(gate0_step, i * G0 + 1)
                    if once(i + 1):
                        mix_blocks(i + 1)
                    dve.max(m80[:], gl0[:]).then_inc(gate0_step, 1)
                    dve.wait_ge(gate0_step, i * G0 + 2)
                    if once(i - 2):
                        turned_low(i - 2)
                    dve.max_index(ix0[:], m80[:], gl0[:]).then_inc(gate0_step, 1)
                    dve.wait_ge(gate0_step, i * G0 + 3)
                    dve.tensor_copy(ixf0[:], ix0[:, 0:1]).then_inc(gate0_step, 1)
                    dve.wait_ge(gate0_step, i * G0 + 4)
                    dve.scalar_tensor_tensor(zm[:], iota_e[:], ixf0[:, 0:1],
                                             ps_up[:, 1, HALF:HALF + Z0].rearrange("p (e r) -> p e r", r=R0),
                                             ALU.is_equal, ALU.mult).then_inc(z_ready, 1)
                    dve.wait_ge(z_ready, i * 3 + 1)
                    after(dve, zt_done, i)
                    dve.tensor_copy(zc[:, 0:3:2], zm[:].rearrange("p e r -> p (e r)").unsqueeze(1)
                                    .to_broadcast([P, 2, Z0])).then_inc(z_ready, 1)
                    dve.wait_ge(z_ready, i * 3 + 2)
                    dve.tensor_tensor(zc[:, 1], zm[:].rearrange("p e r -> p (e r)"), zc[:, 0], ALU.subtract)\
                        .then_inc(z_ready, 1)
                else:
                    if once(i + 1):
                        mix_blocks(i + 1)
                    if once(i - 2):
                        turned_low(i - 2)
                if once(i - 1):
                    dve.wait_ge(conv_done, i)
                    after(dve, clo_done, i - 1)
                    dve.tensor_tensor(c32[:].rearrange("m p (b o) -> m b p o", b=SPT),
                                      ps_conv[:, 0].rearrange("m (b p o) -> m b p o", b=SPT, p=NQ),
                                      rows[:, 1, bass.ds((i - 1) * P, P)].rearrange("m (b o) -> m b o", b=SPT)
                                      .unsqueeze(2).to_broadcast([P, SPT, NQ, C]), ALU.add)\
                        .then_inc(c32_done, 1)
                if once(i - 2):
                    dve.wait_ge(delta_done, i - 1)
                    dve.wait_ge(x1b_done, i - 1)
                    after(dve, stored[par], pair_count(i, par, -4))
                    dve.tensor_tensor(ot[:, par].rearrange("p (j d) -> p j d", j=2), ps_base[:, :, 0:HALF],
                                      x1b[:, par].rearrange("p (j d) -> p j d", j=2), ALU.add)\
                        .then_inc(out_done, 1)
                if once(i + 1):
                    y_sum(i + 1)
                if once(i):
                    dve.wait_ge(lb_done, i + 1)
                    after(dve, xq_in, i * XQ)
                    after(dve, x1b_done, i)
                    dve.tensor_tensor(x1p[:].rearrange("p (j q) m -> p j q m", j=2),
                                      ps_up[:, :, 0:HALF].rearrange("p j (q m) -> p j q m", q=2),
                                      xt[:, par].rearrange("p (m j q) -> p j q m", j=2, q=2), ALU.add)\
                        .then_inc(x1_done, 1)

            iterate(dve, body)

        @block.tensor
        def _(pe):
            pe.wait_ge(ident_ready, 1)
            pe.wait_ge(in_cond, 160)
            pe.transpose(ps_mix[:, 0, 0:P], cond_s[:], ident[:]).then_inc(cond_turned, 1)
            pe.transpose(ps_conv[:, 0, 0:C], wctx_s[:], ident[0:C, 0:C]).then_inc(cond_turned, 1)
            pe.wait_ge(cond_copied, 2)
            pe.matmul(ps_mix[:, 0, 0:P], W0_s[:], condT[:], start=True, stop=True).then_inc(mlp_done, 1)
            pe.matmul(ps_conv[:, 0, 0:C], condT[:], wctxT[:], start=True, stop=True).then_inc(ctx_done, 1)
            pe.wait_ge(wmix_copied, 1)
            for k in range(KATT):
                mm = pe.matmul(ps_h[:, 0, k * C:(k + 1) * C],
                               wmix_rep[:, k].rearrange("o b i -> o (b i)"), ident[0:C, 0:C],
                               start=True, stop=True)
            mm.then_inc(wmix_turned, 1)
            pe.wait_ge(gelu_done, 1)
            pe.matmul(ps_mix[:, 0, 0:P], W1_s[:], h1T[:], start=True, stop=True).then_inc(mlp_done, 1)
            pe.wait_ge(taps_ready, 1 + NQ)
            for s in range(SLOTS):
                mm = pe.matmul(ps_z[:, 0, s * C:(s + 1) * C],
                               taps_q[:, SLOTS - 1 - s].rearrange("o c q -> o (c q)"), ident[0:C, 0:C],
                               start=True, stop=True)
            mm.then_inc(conv_turned, 1)
            pe.wait_ge(gelu_done, 2)
            pe.matmul(ps_mix[:, 0, 0:KATT], h2T[:], W2_s[:], start=True, stop=True).then_inc(mlp_done, 1)

            def fill(n):
                load, blocks, cnt, width, _, _ = fills[n]
                pe.wait_ge(*load)
                after(pe, fill_lo, n - 3)
                for k, src in enumerate(blocks):
                    rows_in_, cols = src.shape[0], width
                    outp = 3 * Z0 if n == LB_FILL else P
                    mm = pe.transpose(FILL_BANKS[n % 4][0:outp, k * cols:(k + 1) * cols], src,
                                      ident[0:rows_in_, 0:rows_in_])
                mm.then_inc(fill_done, 1)

            for n in range(2):
                fill(n)
            pe.wait_ge(att_step, 5)
            pe.transpose(ps_mix[0:KATT, 0, 0:P], att[:], ident[:]).then_inc(att_turned, 1)
            pe.wait_ge(attT_copied, 1)
            pe.matmul(ps_mix[:, 0, 0:C], attT[:], biask_s[:], start=True, stop=True).then_inc(aggb_done, 1)
            pe.wait_ge(spread_ready, 1)
            pe.wait_ge(lane_copied, 1)
            pe.wait_ge(comb_ready, 1)
            pe.matmul(ps_conv[:, 0, 0:NT * KATT], lane_rep[:].rearrange("p j o -> p (j o)"),
                      att_spread[:].rearrange("p t k -> p (t k)"), start=True, stop=True)\
                .then_inc(attb_done, 1)

            def mix(t, par):
                pe.wait_ge(x_in[par], pair_of_x(t, par))
                pe.wait_ge(mixw_done, t + 1)
                after(pe, y32_done, t)
                for k in range(KC):
                    mm = pe.matmul(ps_mix[:, 0, k * P:(k + 1) * P], xt[:, par, k * P:(k + 1) * P],
                                   mix_w[:].rearrange("p b o -> p (b o)"), start=True, stop=True)
                mm.then_inc(mix_done, 1)

            def pair_of_x(t, par):
                return (t - par) * 8 + 16

            for n in range(2, 4):
                fill(n)
            pe.wait_ge(comb_ready, 2)
            mix(0, 0)
            for n in range(4, NF):
                fill(n)
            pe.wait_ge(fill_lo, NF)
            pe.wait_ge(conv_ready, 1)
            pe.wait_ge(consts_ready, 5)

            def body(i, par):
                if once(i):
                    pe.wait_ge(yhi_done, i + 1)
                    after(pe, x1_done, i)
                    for part, (lhs, weights) in enumerate(((y_hi, (up_hi, up_lo)), (y_lo, (up_hi,)))):
                        if part == 1:
                            pe.wait_ge(ylo_done, i + 1)
                        for k in range(KC):
                            for w in weights:
                                first = part == 0 and k == 0 and w is up_hi
                                pe.matmul(ps_up[:, 0, 0:HALF], lhs[:, k], w[:, k, 0:HALF],
                                          start=first, stop=False, skip_group_check=True)
                                mm = pe.matmul(ps_up[:, 1, 0:L0W - HALF], lhs[:, k], w[:, k, HALF:L0W],
                                               start=first, stop=(part == 1 and k == KC - 1),
                                               skip_group_check=True)
                    mm.then_inc(up_done, 1)
                if once(i - 2):
                    pe.wait_ge(hw_done, (i - 1) * 2)
                    after(pe, htlo_done, i - 2)
                    pe.transpose(ps_h[:, 0, 0:P], hw[:].rearrange("p e r -> p (e r)"), ident[:])\
                        .then_inc(ht_done, 1)
                if once(i - 1):
                    pe.wait_ge(xq_in, i * XQ)
                    after(pe, c32_done, i - 1)
                    for b in range(SPT):
                        for n, d in enumerate((-1, 0, 1)):
                            s = NQ - NQ * d
                            mm = pe.matmul(ps_conv[:, 0, b * P:(b + 1) * P], xq[:, b, 1 + d:1 + d + NM],
                                           conv_w[:, s:s + NQ].rearrange("p s o -> p (s o)"),
                                           start=(n == 0), stop=(n == 2))
                    mm.then_inc(conv_done, 1)
                if once(i):
                    pe.wait_ge(z_ready, i * 3 + 3)
                    after(pe, zT_ready, i)
                    pe.transpose(ps_z[0:3 * Z0, 0, 0:P], zc[:].rearrange("p a z -> p (a z)").bitcast(F32),
                                 ident[:]).then_inc(zt_done, 1)
                if once(i - 2):
                    pe.wait_ge(htlo_done, i - 1)
                    for n, (lhs, w) in enumerate(((hT_hi, b1_hi), (hT_hi, b1_lo), (hT_lo, b1_hi))):
                        for j in range(2):
                            mm = pe.matmul(ps_base[:, j, 0:HALF], lhs[:], w[:, j * HALF:(j + 1) * HALF],
                                           start=False, stop=(n == 2), skip_group_check=True)
                    mm.then_inc(delta_done, 1)
                if once(i + 1):
                    mix(i + 1, 1 - par)
                if once(i):
                    pe.wait_ge(zT_ready, i + 1)
                    for j in range(2):
                        mm = pe.matmul(ps_up[:, j, 0:HALF], zT[:], lb_w[:, j * HALF:(j + 1) * HALF],
                                       start=False, stop=True, skip_group_check=True)
                    mm.then_inc(lb_done, 1)
                if once(i - 1):
                    pe.wait_ge(chi_done, i)
                    after(pe, out_done, i - 1)
                    for part, (lhs, weights) in enumerate(((c_hi, (base_hi, base_lo)), (c_lo, (base_hi,)))):
                        if part == 1:
                            pe.wait_ge(clo_done, i)
                        for q in range(NQ):
                            for w in weights:
                                first = part == 0 and q == 0 and w is base_hi
                                for j in range(2):
                                    mm = pe.matmul(ps_base[:, j, 0:L1W], lhs[:, q], w[:, q, j],
                                                   start=first, stop=(part == 1 and q == NQ - 1),
                                                   skip_group_check=True)
                    mm.then_inc(base_done, 1)

            iterate(pe, body)


_INS = ['x', 'cond_128', 'fside_S_0', 'L0_cond_W0', 'L0_cond_b0', 'L0_cond_W1', 'L0_cond_b1', 'L0_cond_W2',
        'L0_cond_b2', 'L0_cond_weight', 'L0_cond_bias_k', 'L0_ffn_W_up', 'L0_ffn_gate_w', 'L0_ffn_expert_bias',
        'L0_ffn_lora_A', 'L0_ffn_lora_B', 'L1_cond_weight', 'L1_cond_c_weight', 'L1_ffn_W_base',
        'L1_ffn_b_base', 'L1_ffn_W_gate', 'L1_ffn_A', 'L1_ffn_B']


def kernel(**inputs):
    import numpy as _np
    import concourse.bacc as _bacc
    from concourse import mybir as _mybir
    from concourse.bass_utils import run_bass_kernel_spmd as _run

    nc = _bacc.Bacc("TRN2", target_bir_lowering=False, num_devices=1)
    arrays, args = {}, []
    for name in _INS:
        a = _np.ascontiguousarray(inputs[name])
        arrays[f"in_{name}"] = a
        args.append(nc.dram_tensor(f"in_{name}", a.shape, _mybir.dt.from_np(a.dtype), kind="ExternalInput").ap())
    out = nc.dram_tensor("out_x", (B, C, H), F32, kind="ExternalOutput")
    adaln_ffn(nc, *args, out.ap())
    return _run(nc, [arrays], core_ids=[0]).results[0]["out_x"]
```

```python
from contextlib import ExitStack

import concourse.bass as bass
from concourse import mybir

ALU = mybir.AluOpType
ACT = mybir.ActivationFunctionType
AX_X = mybir.AxisListType.X
F32 = mybir.dt.float32
F32R = mybir.dt.float32r
U32 = mybir.dt.uint32

P = 128
B = 128
C = 32
H = 512
SPT = P // C
NT = B // SPT
NQ = 4
NM = H // NQ
KC = H // P
E0, R0 = 4, 8
Z0 = E0 * R0
E1, R1 = 8, 16
KATT = 8
TAPS = 9
GROUPS = 4
GC = C // GROUPS
SLOTS = TAPS + NQ - 1
PAD = NM + 2
HALF = H // 2
L0W = H + Z0 + E0
L1W = HALF + E1 + P // 2
XQ = 16 * SPT
EARLY = 4 * P
REST = 3
LOWEST = -3.4028234663852886e38


def adaln_ffn(nc, x, cond, fside, W0, b0, W1, b1, W2, b2, wmix, bias_k, w_up, gate_w,
              ebias, lora_a, lora_b, wconv, wctx, w_base, b_base, w_gate, a1, bb1, out):
    x_rows = x.rearrange("b c h -> (b c) h")
    out_rows = out.rearrange("b c h -> (b c) h")
    rows_dram = nc.dram_tensor("bias_rows", [2, B * C], F32, kind="Internal").ap()

    with ExitStack() as ctx:
        def sb(name, shape, dt=F32):
            return ctx.enter_context(nc.sbuf_tensor(name, shape, dt))

        def sem(name):
            return ctx.enter_context(nc.semaphore(name))

        def bank(name, banks=1):
            return ctx.enter_context(nc.psum_tensor(name, [P, banks, 512], F32))

        ps_mix, ps_conv, ps_z, ps_h = (bank(n) for n in ("ps_mix", "ps_conv", "ps_z", "ps_h"))
        ps_up, ps_base = bank("ps_up", 2), bank("ps_base", 2)

        cond_s, W0_s, W1_s = sb("cond_s", [P, P]), sb("W0_s", [P, P]), sb("W1_s", [P, P])
        W2_s, b0_s, b1_s = sb("W2_s", [P, KATT]), sb("b0_s", [P, 1]), sb("b1_s", [P, 1])
        b2_s, fside_s = sb("b2_s", [P, KATT]), sb("fside_s", [P, C])
        biask_s, wctx_s = sb("biask_s", [KATT, C]), sb("wctx_s", [C, P])
        wmix_s, wconv_s = sb("wmix_s", [C, KATT, C]), sb("wconv_s", [C, GC * TAPS])
        ebias_s, bbase_s = sb("ebias_s", [P, E0]), sb("bbase_s", [P, H])
        wup_raw, wbase_raw = sb("wup_raw", [P, NQ, H]), sb("wbase_raw", [P, KC, H])
        ga_raw, a1_raw, g1_raw = sb("ga_raw", [Z0 + E0, H]), sb("a1_raw", [P, H]), sb("g1_raw", [E1, H])
        lb_raw, b1m_raw = sb("lb_raw", [P, E0, NQ, R0]), sb("b1m_raw", [P, E1, NQ, R1])

        ident = sb("ident", [P, P])
        ones = sb("ones", [P, P])
        quad = sb("quad", [P, SPT])
        lane4 = sb("lane4", [P, SPT])
        tile_of = sb("tile_of", [P, NT])
        group_of = sb("group_of", [C, GROUPS])
        iota8, iota_e = sb("iota8", [P, E1]), sb("iota_e", [P, E0, R0])

        condT, wctxT = sb("condT", [P, P]), sb("wctxT", [P, C])
        h1T, h2T = sb("h1T", [P, P]), sb("h2T", [P, P])
        lg, mx, negm = sb("lg", [P, KATT]), sb("mx", [P, 1]), sb("negm", [P, 1])
        ex, exsum, exrec = sb("ex", [P, KATT]), sb("exsum", [P, 1]), sb("exrec", [P, 1])
        att, attT = sb("att", [P, KATT]), sb("attT", [KATT, P])
        att_spread = sb("att_spread", [P, NT, KATT])
        comb = sb("comb", [P, 2, C])
        att_b = sb("att_b", [P, NT, KATT])
        wmix_t = sb("wmix_t", [P, C, KATT])
        rows = sb("rows", [P, 2, B * C])

        up_hi, up_lo = sb("up_hi", [P, KC, L0W], F32R), sb("up_lo", [P, KC, L0W], F32R)
        base_hi = sb("base_hi", [P, NQ, 2, L1W], F32R)
        base_lo = sb("base_lo", [P, NQ, 2, L1W], F32R)
        lb_w, lb_tmp = sb("lb_w", [3 * Z0, H], F32R), sb("lb_tmp", [3 * Z0, H], F32R)
        b1_hi, b1_lo = sb("b1_hi", [P, H], F32R), sb("b1_lo", [P, H], F32R)
        taps = sb("taps", [C, GROUPS, GC, TAPS + 2 * (NQ - 1)])
        taps_q = sb("taps_q", [C, SLOTS, C, NQ])
        conv_w = sb("conv_w", [P, SLOTS, C])

        wmix_rep = sb("wmix_rep", [C, KATT, SPT, C])
        lane_rep = sb("lane_rep", [P, SPT, C])
        lb_rep = sb("lb_rep", [P, NQ, 3, E0, R0])
        b1m_t = sb("b1m_t", [P, NQ, E1, R1])

        xt = sb("xt", [P, 2, H])
        prod, gsum = sb("prod", [P, C, KATT]), sb("gsum", [P, C])
        mix_w = sb("mix_w", [P, SPT, C])
        y32, y_hi, y_lo = sb("y32", [P, KC, P]), sb("y_hi", [P, KC, P], F32R), sb("y_lo", [P, KC, P], F32R)
        gl0, m80, ix0 = sb("gl0", [P, 8]), sb("m80", [P, 8]), sb("ix0", [P, 8], U32)
        ixf0, zm, zc = sb("ixf0", [P, 1]), sb("zm", [P, E0, R0]), sb("zc", [P, 3, Z0], F32R)
        zT = sb("zT", [3 * Z0, P], F32R)
        x1p = sb("x1p", [P, NQ, NM])
        x1b = sb("x1b", [P, 2, H])
        xq = sb("xq", [P, SPT, PAD])
        c32, c_hi, c_lo = sb("c32", [P, NQ, P]), sb("c_hi", [P, NQ, P], F32R), sb("c_lo", [P, NQ, P], F32R)
        m81, ix1, ixf1 = sb("m81", [P, 8]), sb("ix1", [P, 8], U32), sb("ixf1", [P, 2])
        d2, e2, esum, erec = sb("d2", [P, 2]), sb("e2", [P, 2]), sb("esum", [P, 1]), sb("erec", [P, 1])
        r0, r1, route = sb("r0", [P, E1]), sb("r1", [P, E1]), sb("route", [P, E1])
        hw = sb("hw", [P, E1, R1])
        hT_hi, hT_lo = sb("hT_hi", [P, P], F32R), sb("hT_lo", [P, P], F32R)
        ot = sb("ot", [P, 2, H])

        in_cond, in_mlp = sem("in_cond"), [sem(f"in_mlp{n}") for n in range(3)]
        in_mix, in_bias, in_ctx, in_conv = sem("in_mix"), sem("in_bias"), sem("in_ctx"), sem("in_conv")
        in_rows, in_b1 = sem("in_rows"), sem("in_b1")
        in_up, in_small0, in_base, in_small1 = [sem("in_up0"), sem("in_up1")], sem("in_small0"), sem("in_base"), sem("in_small1")
        x_in = [sem("x_in0"), sem("x_in1")]
        rows_out = [sem("rows_out0"), sem("rows_out1")]
        rows_in = [sem("rows_in0"), sem("rows_in1"), sem("rows_in_rest")]
        xq_in, stored = sem("xq_in"), [sem("stored0"), sem("stored1")]
        ident_zero, ident_ready, consts_ready = sem("ident_zero"), sem("ident_ready"), sem("consts_ready")
        wctx_turned, wctx_copied, table_loaded = sem("wctx_turned"), sem("wctx_copied"), sem("table_loaded")
        masks_ready, taps_zero, taps_ready = sem("masks_ready"), sem("taps_zero"), sem("taps_ready")
        cond_turned, cond_copied = sem("cond_turned"), sem("cond_copied")
        ctx_done, ctx_copied = sem("ctx_done"), sem("ctx_copied")
        mlp_done, gelu_done = sem("mlp_done"), sem("gelu_done")
        att_step, exp_done, att_turned = sem("att_step"), sem("exp_done"), sem("att_turned")
        attT_copied, spread_ready, aggb_done, attb_done = (sem("attT_copied"), sem("spread_ready"),
                                                           sem("aggb_done"), sem("attb_done"))
        aggb_ready, ctx_ready, attb_ready = sem("aggb_ready"), sem("ctx_ready"), sem("attb_ready")
        wmix_turned, wmix_ready, conv_turned, conv_ready = (sem("wmix_turned"), sem("wmix_ready"),
                                                            sem("conv_turned"), sem("conv_ready"))
        wmix_copied, lane_copied, lb_copied, b1_copied = (sem("wmix_copied"), sem("lane_copied"),
                                                          sem("lb_copied"), sem("b1_copied"))
        fill_done, fill_hi, fill_lo = sem("fill_done"), sem("fill_hi"), sem("fill_lo")
        prod_done, gsum_done, mixw_done = sem("prod_done"), sem("gsum_done"), sem("mixw_done")
        mix_done, y32_done, yhi_done, ylo_done = sem("mix_done"), sem("y32_done"), sem("yhi_done"), sem("ylo_done")
        up_done, gate0_step, z_ready, zt_done, zT_ready = (sem("up_done"), sem("gate0_step"), sem("z_ready"),
                                                           sem("zt_done"), sem("zT_ready"))
        lb_done, x1_done, x1b_done = sem("lb_done"), sem("x1_done"), sem("x1b_done")
        conv_done, c32_done, chi_done, clo_done = sem("conv_done"), sem("c32_done"), sem("chi_done"), sem("clo_done")
        base_done, gate1_step, d2_ready, e2_ready, hw_done = (sem("base_done"), sem("gate1_step"), sem("d2_ready"),
                                                              sem("e2_ready"), sem("hw_done"))
        ht_done, hthi_done, htlo_done = sem("ht_done"), sem("hthi_done"), sem("htlo_done")
        delta_done, out_done = sem("delta_done"), sem("out_done")

        fills = []
        for q in range(NQ):
            cols = slice(q * NM, (q + 1) * NM)
            fills.append(((in_up[q * 2 // NQ], 16), [wup_raw[:, q, k * P:(k + 1) * P] for k in range(KC)], KC, NM,
                          up_hi[:, :, cols], up_lo[:, :, cols]))
        ga = [ga_raw[:, k * P:(k + 1) * P] for k in range(KC)]
        fills.append(((in_small0, 48), ga, KC, Z0 + E0, up_hi[:, :, H:L0W], up_lo[:, :, H:L0W]))
        LB_FILL = len(fills)
        fills.append(((lb_copied, 1), [lb_rep[:, q].rearrange("m a e r -> m (a e r)")
                                        for q in range(NQ)], NQ, NM, None, None))
        for q in range(NQ):
            fills.append(((in_base, 32), [wbase_raw[:, dc, q:H:NQ] for dc in range(KC)], KC, P,
                          base_hi[:, q, :, 0:HALF].rearrange("m j (k d) -> m j k d", k=2),
                          base_lo[:, q, :, 0:HALF].rearrange("m j (k d) -> m j k d", k=2)))
        fills.append(((in_small1, 32), [g1_raw[:, q:H:NQ] for q in range(NQ)], NQ, E1,
                      base_hi[:, :, 0, HALF:HALF + E1], base_lo[:, :, 0, HALF:HALF + E1]))
        fills.append(((in_small1, 32), [a1_raw[:, q:H:NQ] for q in range(NQ)], NQ, P,
                      base_hi[:, :, :, HALF + E1:L1W], base_lo[:, :, :, HALF + E1:L1W]))
        fills.append(((b1_copied, 1), [b1m_t[:, q].rearrange("m e r -> m (e r)") for q in range(NQ)], NQ, NM,
                      b1_hi[:].rearrange("p (m q) -> p q m", q=NQ), b1_lo[:].rearrange("p (m q) -> p q m", q=NQ)))
        NF = len(fills)
        NF0 = LB_FILL + 1
        NF1, NF2 = NF0 + 1, NF0 + 5
        bank_of = [ps_up[:, 0], ps_up[:, 1], ps_base[:, 0], ps_base[:, 1], ps_h[:, 0], ps_z[:, 0],
                   ps_base[:, 0], ps_base[:, 1], ps_h[:, 0], ps_conv[:, 0], ps_base[:, 0],
                   ps_base[:, 1], ps_conv[:, 0]]
        bank_free = [None, None, None, None, (wmix_ready, 1), None,
                     (fill_lo, 3), (fill_lo, 4), (fill_lo, 5), (ctx_ready, 1), (fill_lo, 7),
                     (fill_lo, 8), (fill_lo, 10)]
        assert len(bank_of) == len(bank_free) == NF

        def fill_bank(n, parts=P):
            _, _, cnt, width, hi, _ = fills[n]
            v = bank_of[n][0:parts, 0:cnt * width].rearrange("p (k d) -> p k d", k=cnt)
            if hi is not None and len(hi.shape) == 4:
                if hi.shape[2] == 2 and hi.shape[1] == 2:
                    v = v.rearrange("p (j k) d -> p j k d", j=2)
                else:
                    v = v.rearrange("p k (j d) -> p k j d", j=2)
            return v

        def once(tile):
            return not isinstance(tile, int) or 0 <= tile < NT

        def after(eng, sem, count):
            if not isinstance(count, int) or count > 0:
                eng.wait_ge(sem, count)

        FIRST, LAST = 4, NT - 2
        STEPS = NT + 2

        def iterate(eng, body):
            for i in range(FIRST):
                body(i, i % 2)
            with eng.Fori(FIRST // 2, LAST // 2) as pair:
                body(pair * 2, 0)
                body(pair * 2 + 1, 1)
            for i in range(LAST, STEPS):
                body(i, i % 2)

        def pair_count(i, par, off):
            return (i + (off - (par + off) % 2)) * 8 + 16

        block = ctx.enter_context(nc.Block())

        @block.sync
        def _(sp):
            def load_x(t, par):
                sp.dma_start(xt[:, par], x_rows[bass.ds(t * P, P), :]).then_inc(x_in[par], 16)

            def load_base(half):
                k2 = slice(half * KC // 2, (half + 1) * KC // 2)
                sp.dma_start(wbase_raw[:, k2], w_base.rearrange("(k p) h -> p k h", p=P)[:, k2])\
                    .then_inc(in_base, 16)

            sp.dma_start(cond_s[:], cond).then_inc(in_cond, 16)
            sp.dma_start(W0_s[:], W0).then_inc(in_mlp[0], 16)
            sp.dma_start(b0_s[:], b0.rearrange("(p a) -> p a", a=1)).then_inc(in_mlp[0], 16)
            sp.dma_start(W1_s[:], W1).then_inc(in_mlp[1], 16)
            sp.dma_start(b1_s[:], b1.rearrange("(p a) -> p a", a=1)).then_inc(in_mlp[1], 16)
            sp.dma_start(W2_s[:], W2).then_inc(in_mlp[2], 16)
            sp.dma_start(b2_s[:], b2.partition_broadcast(P)).then_inc(in_mlp[2], 16)
            sp.dma_start(biask_s[:], bias_k).then_inc(in_bias, 16)
            sp.dma_start(wmix_s[:], wmix.rearrange("k o i a -> o k (i a)")).then_inc(in_mix, 16)
            for half in range(2):
                q2 = slice(half * NQ // 2, (half + 1) * NQ // 2)
                sp.dma_start(wup_raw[:, q2], w_up.rearrange("(m q) h -> m q h", q=NQ)[:, q2])\
                    .then_inc(in_up[half], 16)
                if half == 0:
                    load_x(0, 0)
            sp.dma_start(wctx_s[:], wctx).then_inc(in_ctx, 16)
            sp.dma_start(fside_s[:], fside.partition_broadcast(P)).then_inc(in_ctx, 16)
            load_base(0)
            sp.wait_ge(aggb_ready, 1)
            sp.dma_start(rows_dram[0].rearrange("(b o) -> b o", b=B), comb[:, 0]).then_inc(rows_out[0], 16)
            load_base(1)
            sp.wait_ge(rows_out[0], 16)
            sp.dma_start(rows[:, 0, 0:EARLY], rows_dram[0, 0:EARLY].partition_broadcast(P))\
                .then_inc(rows_in[0], 16)
            load_x(1, 1)
            sp.dma_start(ebias_s[:], ebias.partition_broadcast(P)).then_inc(in_rows, 16)
            sp.dma_start(g1_raw[:], w_gate).then_inc(in_small1, 16)
            sp.dma_start(a1_raw[:], a1.rearrange("e r d -> (e r) d")).then_inc(in_small1, 16)
            sp.dma_start(bbase_s[:], b_base.partition_broadcast(P)).then_inc(in_rows, 16)
            sp.wait_ge(ctx_ready, 1)
            sp.dma_start(rows_dram[1].rearrange("(b o) -> b o", b=B), comb[:, 1]).then_inc(rows_out[1], 16)
            sp.wait_ge(rows_out[1], 16)
            sp.dma_start(rows[:, 1, 0:EARLY], rows_dram[1, 0:EARLY].partition_broadcast(P))\
                .then_inc(rows_in[1], 16)
            def body(i, par):
                if once(i):
                    sp.wait_ge(x1_done, i + 1)
                    for b in range(SPT):
                        sp.dma_start(xq[:, b, 1:1 + NM], x1p[b * C:(b + 1) * C]).then_inc(xq_in, 16)
                    if not isinstance(i, int) or i + 2 < NT:
                        load_x(i + 2, par)
                if isinstance(i, int) and i < REST:
                    part = (B * C - EARLY) // REST
                    cols = slice(EARLY + i * part, B * C if i == REST - 1 else EARLY + (i + 1) * part)
                    for j in range(2):
                        sp.dma_start(rows[:, j, cols], rows_dram[j, cols].partition_broadcast(P))\
                            .then_inc(rows_in[2], 16)
                if once(i - 2):
                    sp.wait_ge(out_done, i - 1)
                    sp.dma_start(out_rows[bass.ds((i - 2) * P, P), :], ot[:, par]).then_inc(stored[par], 16)

            iterate(sp, body)
            for par in range(2):
                sp.wait_ge(stored[par], 16 * (NT // 2))

        @block.gpsimd
        def _(pool):
            pool.memset(ident[:], 0.0).then_inc(ident_zero, 1)
            pool.wait_ge(ident_zero, 1)
            pool.affine_select(out=ident[:], in_=ident[:], compare_op=ALU.not_equal, fill=1.0, base=0,
                               pattern=[[-1, P]], channel_multiplier=1).then_inc(ident_ready, 1)
            pool.dma_start(ga_raw[0:Z0], lora_a.rearrange("e r h -> (e r) h")).then_inc(in_small0, 16)
            pool.dma_start(ga_raw[Z0:Z0 + E0], gate_w).then_inc(in_small0, 16)
            pool.dma_start(lb_raw[:].rearrange("m e q r -> m e (q r)"),
                           lora_b.rearrange("e (m q) r -> m e (q r)", q=NQ)).then_inc(in_small0, 16)
            pool.dma_start(wconv_s[:], wconv.rearrange("o i k -> o (i k)")).then_inc(in_conv, 16)
            pool.iota(iota8[:], [[1, E1]], base=0, channel_multiplier=0,
                      allow_small_or_imprecise_dtypes=True).then_inc(consts_ready, 1)
            pool.iota(iota_e[:], [[1, E0], [0, R0]], base=0, channel_multiplier=0,
                      allow_small_or_imprecise_dtypes=True).then_inc(consts_ready, 1)
            pool.memset(base_hi[:, :, 1, HALF:HALF + E1].bitcast(F32), 0.0).then_inc(consts_ready, 1)
            pool.memset(base_lo[:, :, 1, HALF:HALF + E1].bitcast(F32), 0.0).then_inc(consts_ready, 1)
            pool.memset(xq[:], 0.0).then_inc(consts_ready, 1)

            def make_prod(t):
                after(pool, gsum_done, t)
                pool.tensor_tensor(prod[:], wmix_t[:], att_b[:, bass.ds(t, 1), :].to_broadcast([P, C, KATT]),
                                   ALU.mult).then_inc(prod_done, 1)

            pool.wait_ge(in_small0, 48)
            for n in range(3):
                cp = pool.tensor_copy(lb_rep[:, :, n], lb_raw[:].rearrange("m e q r -> m q e r"))
            cp.then_inc(lb_copied, 1)
            pool.wait_ge(attb_ready, 1)
            pool.wait_ge(wmix_ready, 1)
            make_prod(0)
            make_prod(1)
            pool.wait_ge(in_conv, 16)
            pool.wait_ge(taps_zero, 1)
            pool.wait_ge(masks_ready, 6)
            pool.tensor_tensor(taps[:, :, :, NQ - 1:NQ - 1 + TAPS],
                               wconv_s[:].rearrange("o (i k) -> o i k", k=TAPS).unsqueeze(1)
                               .to_broadcast([C, GROUPS, GC, TAPS]),
                               group_of[:].unsqueeze(2).unsqueeze(3).to_broadcast([C, GROUPS, GC, TAPS]),
                               ALU.mult).then_inc(taps_ready, 1)
            pool.dma_start(b1m_raw[:].rearrange("m e q r -> m e (q r)"),
                           bb1.rearrange("e (m q) r -> m e (q r)", q=NQ)).then_inc(in_b1, 16)
            pool.wait_ge(y32_done, 1)
            pool.wait_ge(yhi_done, 1)
            pool.tensor_tensor(y_lo[:], y32[:], y_hi[:], ALU.subtract).then_inc(ylo_done, 1)
            pool.wait_ge(in_b1, 16)
            pool.tensor_copy(b1m_t[:], b1m_raw[:].rearrange("m e q r -> m q e r")).then_inc(b1_copied, 1)

            def body(i, par):
                if once(i + 2):
                    make_prod(i + 2)
                if once(i - 1):
                    pool.wait_ge(c32_done, i)
                    pool.wait_ge(chi_done, i)
                    pool.tensor_tensor(c_lo[:], c32[:], c_hi[:], ALU.subtract).then_inc(clo_done, 1)
                if once(i + 1):
                    pool.wait_ge(y32_done, i + 2)
                    pool.wait_ge(yhi_done, i + 2)
                    pool.tensor_tensor(y_lo[:], y32[:], y_hi[:], ALU.subtract).then_inc(ylo_done, 1)
                if isinstance(i, int) and i == 0:
                    pool.wait_ge(in_rows, 32)
                if once(i):
                    pool.wait_ge(x1_done, i + 1)
                    after(pool, out_done, i - 1)
                    pool.tensor_tensor(x1b[:, par].rearrange("p (m q) -> p m q", q=NQ),
                                       x1p[:].rearrange("p q m -> p m q"),
                                       bbase_s[:].rearrange("p (m q) -> p m q", q=NQ),
                                       ALU.add).then_inc(x1b_done, 1)

            iterate(pool, body)

        @block.scalar
        def _(act):
            act.wait_ge(ident_ready, 1)
            act.activation(h1T[:, 0:1], ident[:, 0:1], ACT.Gelu).then_inc(table_loaded, 1)
            act.wait_ge(in_mlp[0], 32)
            act.wait_ge(mlp_done, 1)
            act.wait_ge(table_loaded, 1)
            act.activation(h1T[:], ps_mix[:, 0, 0:P], ACT.Gelu, bias=b0_s[:, 0:1]).then_inc(gelu_done, 1)
            act.wait_ge(in_mlp[1], 32)
            act.wait_ge(mlp_done, 2)
            act.activation(h2T[:], ps_mix[:, 0, 0:P], ACT.Gelu, bias=b1_s[:, 0:1]).then_inc(gelu_done, 1)
            act.activation(ex[:, 0:1], ident[:, 0:1], ACT.Exp).then_inc(table_loaded, 1)

            def high_part(n):
                act.wait_ge(fill_done, n + 1)
                if n == LB_FILL:
                    v = fill_bank(n, 3 * Z0)
                    act.activation(lb_w[0:2 * Z0].rearrange("p (k d) -> p k d", k=NQ), v[0:2 * Z0],
                                   ACT.Copy).then_inc(fill_hi, 1)
                    act.activation(lb_tmp[2 * Z0:].rearrange("p (k d) -> p k d", k=NQ), v[2 * Z0:],
                                   ACT.Copy).then_inc(fill_hi, 1)
                else:
                    act.activation(fills[n][4], fill_bank(n), ACT.Copy).then_inc(fill_hi, 1)

            def y_high(t):
                act.wait_ge(y32_done, t + 1)
                act.activation(y_hi[:], y32[:], ACT.Copy).then_inc(yhi_done, 1)

            act.wait_ge(att_step, 3)
            act.wait_ge(table_loaded, 2)
            act.activation(ex[:], lg[:], ACT.Exp, bias=negm[:, 0:1], accum_out=exsum[:, 0:1]).then_inc(exp_done, 1)
            for n in range(LB_FILL):
                high_part(n)
            y_high(0)
            for n in range(LB_FILL, NF1):
                high_part(n)

            def body(i, par):
                if once(i - 2):
                    act.wait_ge(d2_ready, i - 1)
                    act.activation(e2[:], d2[:], ACT.Exp, accum_out=esum[:, 0:1]).then_inc(e2_ready, 1)
                    act.wait_ge(ht_done, i - 1)
                    act.activation(hT_hi[:], ps_h[:, 0, 0:P], ACT.Copy).then_inc(hthi_done, 1)
                if isinstance(i, int) and i == 0:
                    for n in range(NF1, NF2):
                        high_part(n)
                if once(i):
                    act.wait_ge(zt_done, i + 1)
                    act.activation(zT[:], ps_z[0:3 * Z0, 0, 0:P], ACT.Copy).then_inc(zT_ready, 1)
                if once(i - 1):
                    act.wait_ge(c32_done, i)
                    act.activation(c_hi[:], c32[:], ACT.Copy).then_inc(chi_done, 1)
                if once(i + 1):
                    y_high(i + 1)
                if isinstance(i, int) and i == 0:
                    for n in range(NF2, NF):
                        high_part(n)

            iterate(act, body)

        @block.vector
        def _(dve):
            dve.wait_ge(ident_ready, 1)
            dve.memset(ones[:], 1.0).then_inc(masks_ready, 1)
            dve.tensor_reduce(quad[:], ident[:].rearrange("p (j r) -> p j r", j=SPT), AX_X, ALU.add)\
                .then_inc(masks_ready, 1)
            dve.tensor_reduce(lane4[:], ident[:].rearrange("p (t j) -> p j t", j=SPT), AX_X, ALU.add)\
                .then_inc(masks_ready, 1)
            dve.tensor_reduce(tile_of[:], ident[:].rearrange("p (t j) -> p t j", j=SPT), AX_X, ALU.add)\
                .then_inc(masks_ready, 1)
            dve.tensor_reduce(group_of[:], ident[0:C, 0:C].rearrange("p (g r) -> p g r", g=GROUPS), AX_X, ALU.add)\
                .then_inc(masks_ready, 1)
            dve.memset(gl0[:], LOWEST).then_inc(masks_ready, 1)
            dve.memset(taps[:], 0.0).then_inc(taps_zero, 1)

            def low_part(n):
                dve.wait_ge(fill_hi, n + 1 + (n >= LB_FILL))
                if n == LB_FILL:
                    dve.tensor_tensor(lb_w[2 * Z0:].rearrange("p (k d) -> p k d", k=NQ),
                                      fill_bank(n, 3 * Z0)[2 * Z0:],
                                      lb_tmp[2 * Z0:].rearrange("p (k d) -> p k d", k=NQ),
                                      ALU.subtract).then_inc(fill_lo, 1)
                else:
                    dve.tensor_tensor(fills[n][5], fill_bank(n), fills[n][4], ALU.subtract).then_inc(fill_lo, 1)

            def mix_sums(t):
                dve.wait_ge(prod_done, t + 1)
                dve.tensor_reduce(gsum[:], prod[:], AX_X, ALU.add).then_inc(gsum_done, 1)

            def mix_blocks(t):
                dve.wait_ge(gsum_done, t + 1)
                after(dve, mix_done, t)
                dve.tensor_tensor(mix_w[:], gsum[:].unsqueeze(1).to_broadcast([P, SPT, C]),
                                  quad[:].unsqueeze(2).to_broadcast([P, SPT, C]), ALU.mult)\
                    .then_inc(mixw_done, 1)

            def y_sum(t):
                if isinstance(t, int) and t == EARLY // P:
                    dve.wait_ge(rows_in[2], 32 * REST)
                dve.wait_ge(mix_done, t + 1)
                after(dve, ylo_done, t)
                dve.tensor_tensor(y32[:], ps_mix[:, 0].rearrange("p (k r) -> p k r", k=KC),
                                  rows[:, 0, bass.ds(t * P, P)].unsqueeze(1).to_broadcast([P, KC, P]),
                                  ALU.add).then_inc(y32_done, 1)

            dve.wait_ge(cond_turned, 1)
            dve.tensor_copy(condT[:], ps_mix[:, 0, 0:P]).then_inc(cond_copied, 1)
            dve.wait_ge(in_mix, 16)
            dve.tensor_copy(wmix_rep[:], wmix_s[:].unsqueeze(2).to_broadcast([C, KATT, SPT, C]))\
                .then_inc(wmix_copied, 1)
            dve.wait_ge(masks_ready, 6)
            dve.tensor_copy(lane_rep[:], lane4[:].unsqueeze(2).to_broadcast([P, SPT, C])).then_inc(lane_copied, 1)
            dve.wait_ge(in_mlp[2], 32)
            dve.wait_ge(mlp_done, 3)
            dve.tensor_tensor(lg[:], ps_mix[:, 0, 0:KATT], b2_s[:], ALU.add).then_inc(att_step, 1)
            dve.wait_ge(att_step, 1)
            dve.reduce_max(mx[:], lg[:], AX_X).then_inc(att_step, 1)
            dve.wait_ge(att_step, 2)
            dve.tensor_scalar(negm[:], mx[:], -1.0, None, ALU.mult).then_inc(att_step, 1)
            dve.wait_ge(exp_done, 1)
            dve.reciprocal(exrec[:], exsum[:]).then_inc(att_step, 1)
            dve.wait_ge(att_step, 4)
            dve.tensor_scalar(att[:], ex[:], exrec[:, 0:1], None, ALU.mult).then_inc(att_step, 1)
            dve.wait_ge(att_step, 5)
            dve.wait_ge(masks_ready, 6)
            dve.tensor_tensor(att_spread[:], tile_of[:].unsqueeze(2).to_broadcast([P, NT, KATT]),
                              att[:].unsqueeze(1).to_broadcast([P, NT, KATT]), ALU.mult)\
                .then_inc(spread_ready, 1)
            dve.wait_ge(att_turned, 1)
            dve.tensor_copy(attT[:], ps_mix[0:KATT, 0, 0:P]).then_inc(attT_copied, 1)
            dve.wait_ge(aggb_done, 1)
            dve.tensor_copy(comb[:, 0], ps_mix[:, 0, 0:C]).then_inc(aggb_ready, 1)
            dve.wait_ge(wmix_turned, 1)
            dve.tensor_copy(wmix_t[:], ps_h[:, 0, 0:KATT * C].rearrange("p (k o) -> p o k", k=KATT))\
                .then_inc(wmix_ready, 1)
            dve.wait_ge(attb_done, 1)
            dve.tensor_copy(att_b[:], ps_conv[:, 0, 0:NT * KATT].rearrange("p (t k) -> p t k", k=KATT))\
                .then_inc(attb_ready, 1)
            mix_sums(0)
            mix_blocks(0)
            low_part(0)
            low_part(1)
            dve.wait_ge(wctx_turned, 1)
            dve.tensor_copy(wctxT[:], ps_conv[:, 0, 0:C]).then_inc(wctx_copied, 1)
            low_part(2)
            dve.wait_ge(ctx_done, 1)
            dve.wait_ge(in_ctx, 32)
            dve.tensor_tensor(comb[:, 1], ps_conv[:, 0, 0:C], fside_s[:], ALU.add).then_inc(ctx_ready, 1)
            dve.wait_ge(rows_in[0], 16)
            y_sum(0)
            for n in range(3, NF1):
                low_part(n)
            dve.wait_ge(taps_ready, 1)
            for q in range(NQ):
                dve.tensor_copy(taps_q[:, :, :, q],
                                taps[:, :, :, q:q + SLOTS].rearrange("o g i s -> o s (g i)"))\
                    .then_inc(taps_ready, 1)
            dve.wait_ge(in_rows, 32)

            def late_parts():
                dve.wait_ge(conv_turned, 1)
                dve.tensor_copy(conv_w[:], ps_h[:, 0, 0:SLOTS * C].rearrange("p (s o) -> p s o", s=SLOTS))\
                    .then_inc(conv_ready, 1)
                for n in range(NF2, NF):
                    low_part(n)

            def turned_low(t):
                dve.wait_ge(hthi_done, t + 1)
                dve.tensor_tensor(hT_lo[:], ps_h[:, 0, 0:P], hT_hi[:], ALU.subtract).then_inc(htlo_done, 1)

            G1 = 6
            G0 = 4

            def body(i, par):
                if once(i - 2):
                    t = i - 2
                    logits = ps_base[:, 0, HALF:HALF + E1]
                    dve.wait_ge(base_done, t + 1)
                    if once(i + 1):
                        mix_sums(i + 1)
                    dve.max(m81[:], logits).then_inc(gate1_step, 1)
                    dve.wait_ge(gate1_step, t * G1 + 1)
                    dve.tensor_scalar(d2[:], m81[:, 0:2], m81[:, 0:1], None, ALU.subtract).then_inc(d2_ready, 1)
                    dve.max_index(ix1[:], m81[:], logits).then_inc(gate1_step, 1)
                    dve.wait_ge(gate1_step, t * G1 + 2)
                    dve.tensor_copy(ixf1[:], ix1[:, 0:2]).then_inc(gate1_step, 1)
                    dve.wait_ge(e2_ready, t + 1)
                    dve.reciprocal(erec[:], esum[:]).then_inc(gate1_step, 1)
                    dve.wait_ge(gate1_step, t * G1 + 3)
                    dve.tensor_scalar(r0[:], iota8[:], ixf1[:, 0:1], e2[:, 0:1], ALU.is_equal, ALU.mult)
                    dve.tensor_scalar(r1[:], iota8[:], ixf1[:, 1:2], e2[:, 1:2], ALU.is_equal, ALU.mult)\
                        .then_inc(gate1_step, 1)
                    dve.wait_ge(gate1_step, t * G1 + 5)
                    dve.tensor_tensor(route[:], r0[:], r1[:], ALU.add).then_inc(gate1_step, 1)
                    dve.wait_ge(gate1_step, t * G1 + 6)
                    after(dve, ht_done, t)
                    for j in range(2):
                        e = slice(j * E1 // 2, (j + 1) * E1 // 2)
                        dve.scalar_tensor_tensor(
                            hw[:, e], ps_base[:, j, HALF + E1:L1W].rearrange("p (e r) -> p e r", r=R1),
                            erec[:, 0:1], route[:, e].unsqueeze(2).to_broadcast([P, E1 // 2, R1]),
                            ALU.mult, ALU.mult).then_inc(hw_done, 1)
                elif once(i + 1):
                    mix_sums(i + 1)
                if once(i):
                    dve.wait_ge(up_done, i + 1)
                    dve.tensor_tensor(gl0[:, 0:E0], ps_up[:, 1, HALF + Z0:HALF + Z0 + E0], ebias_s[:], ALU.add)\
                        .then_inc(gate0_step, 1)
                    dve.wait_ge(gate0_step, i * G0 + 1)
                    if once(i + 1):
                        mix_blocks(i + 1)
                    dve.max(m80[:], gl0[:]).then_inc(gate0_step, 1)
                    dve.wait_ge(gate0_step, i * G0 + 2)
                    if once(i - 2):
                        turned_low(i - 2)
                    dve.max_index(ix0[:], m80[:], gl0[:]).then_inc(gate0_step, 1)
                    dve.wait_ge(gate0_step, i * G0 + 3)
                    dve.tensor_copy(ixf0[:], ix0[:, 0:1]).then_inc(gate0_step, 1)
                    dve.wait_ge(gate0_step, i * G0 + 4)
                    dve.scalar_tensor_tensor(zm[:], iota_e[:], ixf0[:, 0:1],
                                             ps_up[:, 1, HALF:HALF + Z0].rearrange("p (e r) -> p e r", r=R0),
                                             ALU.is_equal, ALU.mult).then_inc(z_ready, 1)
                    dve.wait_ge(z_ready, i * 3 + 1)
                    after(dve, zt_done, i)
                    dve.tensor_copy(zc[:, 0:3:2], zm[:].rearrange("p e r -> p (e r)").unsqueeze(1)
                                    .to_broadcast([P, 2, Z0])).then_inc(z_ready, 1)
                    dve.wait_ge(z_ready, i * 3 + 2)
                    dve.tensor_tensor(zc[:, 1], zm[:].rearrange("p e r -> p (e r)"), zc[:, 0], ALU.subtract)\
                        .then_inc(z_ready, 1)
                else:
                    if once(i + 1):
                        mix_blocks(i + 1)
                    if once(i - 2):
                        turned_low(i - 2)
                if isinstance(i, int) and i == 0:
                    for n in range(NF1, NF2):
                        low_part(n)
                if once(i - 1):
                    if isinstance(i, int) and i == 1:
                        dve.wait_ge(rows_in[1], 16)
                    dve.wait_ge(conv_done, i)
                    after(dve, clo_done, i - 1)
                    dve.tensor_tensor(c32[:].rearrange("m p (b o) -> m b p o", b=SPT),
                                      ps_conv[:, 0].rearrange("m (b p o) -> m b p o", b=SPT, p=NQ),
                                      rows[:, 1, bass.ds((i - 1) * P, P)].rearrange("m (b o) -> m b o", b=SPT)
                                      .unsqueeze(2).to_broadcast([P, SPT, NQ, C]), ALU.add)\
                        .then_inc(c32_done, 1)
                if once(i - 2):
                    dve.wait_ge(delta_done, i - 1)
                    dve.wait_ge(x1b_done, i - 1)
                    after(dve, stored[par], pair_count(i, par, -4))
                    dve.tensor_tensor(ot[:, par].rearrange("p (j d) -> p j d", j=2), ps_base[:, :, 0:HALF],
                                      x1b[:, par].rearrange("p (j d) -> p j d", j=2), ALU.add)\
                        .then_inc(out_done, 1)
                if once(i + 1):
                    y_sum(i + 1)
                if once(i):
                    dve.wait_ge(lb_done, i + 1)
                    after(dve, xq_in, i * XQ)
                    after(dve, x1b_done, i)
                    dve.tensor_tensor(x1p[:].rearrange("p (j q) m -> p j q m", j=2),
                                      ps_up[:, :, 0:HALF].rearrange("p j (q m) -> p j q m", q=2),
                                      xt[:, par].rearrange("p (m j q) -> p j q m", j=2, q=2), ALU.add)\
                        .then_inc(x1_done, 1)
                if isinstance(i, int) and i == 0:
                    late_parts()

            iterate(dve, body)

        @block.tensor
        def _(pe):
            pe.wait_ge(ident_ready, 1)

            def fill(n):
                load, blocks, cnt, width, _, _ = fills[n]
                pe.wait_ge(*load)
                if bank_free[n]:
                    pe.wait_ge(*bank_free[n])
                for k, src in enumerate(blocks):
                    rows_in_, cols = src.shape[0], width
                    outp = 3 * Z0 if n == LB_FILL else P
                    mm = pe.transpose(bank_of[n][0:outp, k * cols:(k + 1) * cols], src,
                                      ident[0:rows_in_, 0:rows_in_])
                mm.then_inc(fill_done, 1)

            pe.wait_ge(in_cond, 16)
            pe.transpose(ps_mix[:, 0, 0:P], cond_s[:], ident[:]).then_inc(cond_turned, 1)
            pe.wait_ge(in_mlp[0], 32)
            pe.wait_ge(cond_copied, 1)
            pe.matmul(ps_mix[:, 0, 0:P], W0_s[:], condT[:], start=True, stop=True).then_inc(mlp_done, 1)
            pe.wait_ge(in_mlp[1], 32)
            pe.wait_ge(gelu_done, 1)
            pe.matmul(ps_mix[:, 0, 0:P], W1_s[:], h1T[:], start=True, stop=True).then_inc(mlp_done, 1)
            pe.wait_ge(in_mlp[2], 32)
            pe.wait_ge(gelu_done, 2)
            pe.matmul(ps_mix[:, 0, 0:KATT], h2T[:], W2_s[:], start=True, stop=True).then_inc(mlp_done, 1)
            pe.wait_ge(wmix_copied, 1)
            for k in range(KATT):
                mm = pe.transpose(ps_h[:, 0, k * C:(k + 1) * C],
                                  wmix_rep[:, k].rearrange("o b i -> o (b i)"), ident[0:C, 0:C])
            mm.then_inc(wmix_turned, 1)
            pe.wait_ge(att_step, 5)
            pe.transpose(ps_mix[0:KATT, 0, 0:P], att[:], ident[:]).then_inc(att_turned, 1)
            pe.wait_ge(in_bias, 16)
            pe.wait_ge(attT_copied, 1)
            pe.matmul(ps_mix[:, 0, 0:C], attT[:], biask_s[:], start=True, stop=True).then_inc(aggb_done, 1)
            pe.wait_ge(spread_ready, 1)
            pe.wait_ge(lane_copied, 1)
            pe.matmul(ps_conv[:, 0, 0:NT * KATT], lane_rep[:].rearrange("p j o -> p (j o)"),
                      att_spread[:].rearrange("p t k -> p (t k)"), start=True, stop=True)\
                .then_inc(attb_done, 1)

            def turn_hw(t):
                pe.wait_ge(hw_done, (t + 1) * 2)
                after(pe, htlo_done, t)
                pe.transpose(ps_h[:, 0, 0:P], hw[:].rearrange("p e r -> p (e r)"), ident[:])\
                    .then_inc(ht_done, 1)

            def mix(t, par):
                pe.wait_ge(x_in[par], pair_of_x(t, par))
                pe.wait_ge(mixw_done, t + 1)
                after(pe, y32_done, t)
                for k in range(KC):
                    mm = pe.matmul(ps_mix[:, 0, k * P:(k + 1) * P], xt[:, par, k * P:(k + 1) * P],
                                   mix_w[:].rearrange("p b o -> p (b o)"), start=True, stop=True)
                mm.then_inc(mix_done, 1)

            def pair_of_x(t, par):
                return (t - par) * 8 + 16

            fill(0)
            fill(1)
            pe.wait_ge(in_ctx, 32)
            pe.wait_ge(attb_ready, 1)
            pe.transpose(ps_conv[:, 0, 0:C], wctx_s[:], ident[0:C, 0:C]).then_inc(wctx_turned, 1)
            fill(2)
            pe.wait_ge(aggb_ready, 1)
            mix(0, 0)
            pe.wait_ge(wctx_copied, 1)
            pe.matmul(ps_conv[:, 0, 0:C], condT[:], wctxT[:], start=True, stop=True).then_inc(ctx_done, 1)
            for n in range(3, NF1):
                fill(n)
            pe.wait_ge(fill_lo, LB_FILL)

            def turn_taps():
                pe.wait_ge(taps_ready, 1 + NQ)
                pe.wait_ge(fill_lo, 9)
                for s in range(SLOTS):
                    mm = pe.transpose(ps_h[:, 0, s * C:(s + 1) * C],
                                      taps_q[:, SLOTS - 1 - s].rearrange("o c q -> o (c q)"), ident[0:C, 0:C])
                mm.then_inc(conv_turned, 1)

            def body(i, par):
                if once(i):
                    pe.wait_ge(yhi_done, i + 1)
                    after(pe, x1_done, i)
                    for part, (lhs, weights) in enumerate(((y_hi, (up_hi, up_lo)), (y_lo, (up_hi,)))):
                        if part == 1:
                            pe.wait_ge(ylo_done, i + 1)
                        for k in range(KC):
                            for w in weights:
                                first = part == 0 and k == 0 and w is up_hi
                                pe.matmul(ps_up[:, 0, 0:HALF], lhs[:, k], w[:, k, 0:HALF],
                                          start=first, stop=False, skip_group_check=True)
                                mm = pe.matmul(ps_up[:, 1, 0:L0W - HALF], lhs[:, k], w[:, k, HALF:L0W],
                                               start=first, stop=(part == 1 and k == KC - 1),
                                               skip_group_check=True)
                    mm.then_inc(up_done, 1)
                if isinstance(i, int) and i == 0:
                    for n in range(NF1, NF2):
                        fill(n)
                    pe.wait_ge(fill_lo, NF0)
                if isinstance(i, int) and i == 1:
                    pe.wait_ge(consts_ready, 5)
                    pe.wait_ge(conv_ready, 1)
                    pe.wait_ge(fill_lo, NF)
                last = isinstance(i, int) and i >= NT
                if once(i - 2) and not last:
                    turn_hw(i - 2)
                if once(i - 1):
                    pe.wait_ge(xq_in, i * XQ)
                    after(pe, c32_done, i - 1)
                    for b in range(SPT):
                        for n, d in enumerate((-1, 0, 1)):
                            s = NQ - NQ * d
                            mm = pe.matmul(ps_conv[:, 0, b * P:(b + 1) * P], xq[:, b, 1 + d:1 + d + NM],
                                           conv_w[:, s:s + NQ].rearrange("p s o -> p (s o)"),
                                           start=(n == 0), stop=(n == 2))
                    mm.then_inc(conv_done, 1)
                if once(i - 2) and last:
                    turn_hw(i - 2)
                if once(i):
                    pe.wait_ge(z_ready, i * 3 + 3)
                    after(pe, zT_ready, i)
                    pe.transpose(ps_z[0:3 * Z0, 0, 0:P], zc[:].rearrange("p a z -> p (a z)").bitcast(F32),
                                 ident[:]).then_inc(zt_done, 1)
                if once(i - 2):
                    pe.wait_ge(htlo_done, i - 1)
                    for n, (lhs, w) in enumerate(((hT_hi, b1_hi), (hT_hi, b1_lo), (hT_lo, b1_hi))):
                        for j in range(2):
                            mm = pe.matmul(ps_base[:, j, 0:HALF], lhs[:], w[:, j * HALF:(j + 1) * HALF],
                                           start=False, stop=(n == 2), skip_group_check=True)
                    mm.then_inc(delta_done, 1)
                if once(i + 1):
                    mix(i + 1, 1 - par)
                if once(i):
                    pe.wait_ge(zT_ready, i + 1)
                    for j in range(2):
                        mm = pe.matmul(ps_up[:, j, 0:HALF], zT[:], lb_w[:, j * HALF:(j + 1) * HALF],
                                       start=False, stop=True, skip_group_check=True)
                    mm.then_inc(lb_done, 1)
                if isinstance(i, int) and i == 0:
                    turn_taps()
                    for n in range(NF2, NF):
                        fill(n)
                if once(i - 1):
                    pe.wait_ge(chi_done, i)
                    after(pe, out_done, i - 1)
                    for part, (lhs, weights) in enumerate(((c_hi, (base_hi, base_lo)), (c_lo, (base_hi,)))):
                        if part == 1:
                            pe.wait_ge(clo_done, i)
                        for q in range(NQ):
                            for w in weights:
                                first = part == 0 and q == 0 and w is base_hi
                                for j in range(2):
                                    mm = pe.matmul(ps_base[:, j, 0:L1W], lhs[:, q], w[:, q, j],
                                                   start=first, stop=(part == 1 and q == NQ - 1),
                                                   skip_group_check=True)
                    mm.then_inc(base_done, 1)

            iterate(pe, body)


_INS = ['x', 'cond_128', 'fside_S_0', 'L0_cond_W0', 'L0_cond_b0', 'L0_cond_W1', 'L0_cond_b1', 'L0_cond_W2',
        'L0_cond_b2', 'L0_cond_weight', 'L0_cond_bias_k', 'L0_ffn_W_up', 'L0_ffn_gate_w', 'L0_ffn_expert_bias',
        'L0_ffn_lora_A', 'L0_ffn_lora_B', 'L1_cond_weight', 'L1_cond_c_weight', 'L1_ffn_W_base',
        'L1_ffn_b_base', 'L1_ffn_W_gate', 'L1_ffn_A', 'L1_ffn_B']


def kernel(**inputs):
    import numpy as _np
    import concourse.bacc as _bacc
    from concourse import mybir as _mybir
    from concourse.bass_utils import run_bass_kernel_spmd as _run

    nc = _bacc.Bacc("TRN2", target_bir_lowering=False, num_devices=1)
    arrays, args = {}, []
    for name in _INS:
        a = _np.ascontiguousarray(inputs[name])
        arrays[f"in_{name}"] = a
        args.append(nc.dram_tensor(f"in_{name}", a.shape, _mybir.dt.from_np(a.dtype), kind="ExternalInput").ap())
    out = nc.dram_tensor("out_x", (B, C, H), F32, kind="ExternalOutput")
    adaln_ffn(nc, *args, out.ap())
    return _run(nc, [arrays], core_ids=[0]).results[0]["out_x"]
```

```python
from contextlib import ExitStack

import concourse.bass as bass
from concourse import mybir

ALU = mybir.AluOpType
ACT = mybir.ActivationFunctionType
AX_X = mybir.AxisListType.X
F32 = mybir.dt.float32
F32R = mybir.dt.float32r
U32 = mybir.dt.uint32

P = 128
B = 128
C = 32
H = 512
SPT = P // C
NT = B // SPT
NQ = 4
NM = H // NQ
KC = H // P
E0, R0 = 4, 8
Z0 = E0 * R0
E1, R1 = 8, 16
KATT = 8
TAPS = 9
GROUPS = 4
GC = C // GROUPS
SLOTS = TAPS + NQ - 1
PAD = NM + 2
HALF = H // 2
L0W = H + Z0 + E0
L1W = HALF + P + E1
XQ = 16 * SPT
EARLY = 4 * P
REST = 3
LOWEST = -3.4028234663852886e38


def adaln_ffn(nc, x, cond, fside, W0, b0, W1, b1, W2, b2, wmix, bias_k, w_up, gate_w,
              ebias, lora_a, lora_b, wconv, wctx, w_base, b_base, w_gate, a1, bb1, out):
    x_rows = x.rearrange("b c h -> (b c) h")
    out_rows = out.rearrange("b c h -> (b c) h")
    rows_dram = nc.dram_tensor("agg_rows", [B * C], F32, kind="Internal").ap()

    with ExitStack() as ctx:
        def sb(name, shape, dt=F32):
            return ctx.enter_context(nc.sbuf_tensor(name, shape, dt))

        def sem(name):
            return ctx.enter_context(nc.semaphore(name))

        def bank(name, banks=1):
            return ctx.enter_context(nc.psum_tensor(name, [P, banks, 512], F32))

        ps_mix, ps_conv, ps_turn, ps_ct = (bank(n) for n in ("ps_mix", "ps_conv", "ps_turn", "ps_ct"))
        ps_up, ps_base = bank("ps_up", 2), bank("ps_base", 2)

        cond_s, W0_s, W1_s = sb("cond_s", [P, P]), sb("W0_s", [P, P]), sb("W1_s", [P, P])
        W2_s, b0_s, b1_s = sb("W2_s", [P, KATT]), sb("b0_s", [P, 1]), sb("b1_s", [P, 1])
        b2_s, fside_s = sb("b2_s", [P, KATT]), sb("fside_s", [P, 1])
        biask_s, wctx_s = sb("biask_s", [KATT, C]), sb("wctx_s", [C, P])
        wmix_s, wconv_s = sb("wmix_s", [C, KATT, C]), sb("wconv_s", [C, GC * TAPS])
        ebias_s, bbase_s = sb("ebias_s", [P, E0]), sb("bbase_s", [P, H])
        wup_raw, wbase_raw = sb("wup_raw", [P, NQ, H]), sb("wbase_raw", [P, KC, H])
        ga_raw, a1_raw, g1_raw = sb("ga_raw", [Z0 + E0, H]), sb("a1_raw", [P, H]), sb("g1_raw", [E1, H])
        lb_raw, b1m_raw = sb("lb_raw", [P, E0, NQ, R0]), sb("b1m_raw", [P, E1, NQ, R1])

        ident = sb("ident", [P, P])
        quad = sb("quad", [P, SPT])
        lane4 = sb("lane4", [P, SPT])
        tile_of = sb("tile_of", [P, NT])
        group_of = sb("group_of", [C, GROUPS])
        iota8, iota_e = sb("iota8", [P, E1]), sb("iota_e", [P, E0, R0])

        condT, wctxT = sb("condT", [P, P]), sb("wctxT", [P, NQ, C])
        h1T, h2T = sb("h1T", [P, P]), sb("h2T", [P, P])
        lg, mx, negm = sb("lg", [P, KATT]), sb("mx", [P, 1]), sb("negm", [P, 1])
        ex, exsum, exrec = sb("ex", [P, KATT]), sb("exsum", [P, 1]), sb("exrec", [P, 1])
        att, attT = sb("att", [P, KATT]), sb("attT", [KATT, P])
        att_spread = sb("att_spread", [P, NT, KATT])
        agg_b = sb("agg_b", [P, C])
        biasT = sb("biasT", [P, B])
        att_b = sb("att_b", [P, NT, KATT])
        wmix_t = sb("wmix_t", [P, C, KATT])
        rows = sb("rows", [P, B * C])

        up_hi, up_lo = sb("up_hi", [P, KC, L0W], F32R), sb("up_lo", [P, KC, L0W], F32R)
        base_hi = sb("base_hi", [P, NQ, 2, L1W], F32R)
        base_lo = sb("base_lo", [P, NQ, 2, L1W], F32R)
        lb_w, lb_tmp = sb("lb_w", [3 * Z0, H], F32R), sb("lb_tmp", [3 * Z0, H], F32R)
        b1_hi, b1_lo = sb("b1_hi", [P, H], F32R), sb("b1_lo", [P, H], F32R)
        taps = sb("taps", [C, GROUPS, GC, TAPS + 2 * (NQ - 1)])
        taps_q = sb("taps_q", [C, SLOTS, C, NQ])
        conv_hi, conv_lo = sb("conv_hi", [P, SLOTS, C], F32R), sb("conv_lo", [P, SLOTS, C], F32R)

        wmix_rep = sb("wmix_rep", [C, KATT, SPT, C])
        lane_rep = sb("lane_rep", [P, SPT, C])
        lb_rep = sb("lb_rep", [P, NQ, 3, E0, R0])
        b1m_t = sb("b1m_t", [P, NQ, E1, R1])

        xt = sb("xt", [P, 2, H])
        prod, gsum = sb("prod", [P, C, KATT]), sb("gsum", [P, C])
        mix_w = sb("mix_w", [P, SPT, C])
        y32, y_hi, y_lo = sb("y32", [P, KC, P]), sb("y_hi", [P, KC, P], F32R), sb("y_lo", [P, KC, P], F32R)
        gl0, m80, ix0 = sb("gl0", [P, 8]), sb("m80", [P, 8]), sb("ix0", [P, 8], U32)
        ixf0, zm, zc = sb("ixf0", [P, 1]), sb("zm", [P, E0, R0]), sb("zc", [P, 3, Z0], F32R)
        zT = sb("zT", [3 * Z0, P], F32R)
        x1p = sb("x1p", [P, NQ, NM])
        x1b = sb("x1b", [P, 2, H])
        xq = sb("xq", [P, SPT, PAD])
        xq_hi, xq_lo = sb("xq_hi", [P, SPT, PAD], F32R), sb("xq_lo", [P, SPT, PAD], F32R)
        c32, c_hi, c_lo = sb("c32", [P, SPT, NM]), sb("c_hi", [P, NQ, P], F32R), sb("c_lo", [P, NQ, P], F32R)
        m81, ix1, ixf1 = sb("m81", [P, 8]), sb("ix1", [P, 8], U32), sb("ixf1", [P, 2])
        d2, e2, esum, erec = sb("d2", [P, 2]), sb("e2", [P, 2]), sb("esum", [P, 1]), sb("erec", [P, 1])
        r0, r1, route = sb("r0", [P, E1]), sb("r1", [P, E1]), sb("route", [P, E1])
        hw = sb("hw", [P, E1, R1])
        hT_hi, hT_lo = sb("hT_hi", [P, P], F32R), sb("hT_lo", [P, P], F32R)
        ot = sb("ot", [P, 2, H])

        in_cond, in_mlp = sem("in_cond"), [sem(f"in_mlp{n}") for n in range(3)]
        in_mix, in_bias, in_ctx, in_conv = sem("in_mix"), sem("in_bias"), sem("in_ctx"), sem("in_conv")
        in_rows, in_b1 = sem("in_rows"), sem("in_b1")
        in_up, in_base = [sem("in_up0"), sem("in_up1")], sem("in_base")
        in_small0, in_a1, in_fside, in_gate = sem("in_small0"), sem("in_a1"), sem("in_fside"), sem("in_gate")
        x_in = [sem("x_in0"), sem("x_in1")]
        rows_out, rows_in = sem("rows_out"), [sem("rows_in0"), sem("rows_in_rest")]
        xq_in, stored = sem("xq_in"), [sem("stored0"), sem("stored1")]
        ident_zero, ident_ready, consts_ready = sem("ident_zero"), sem("ident_ready"), sem("consts_ready")
        wctx_turned, wctx_copied, table_loaded = sem("wctx_turned"), sem("wctx_copied"), sem("table_loaded")
        masks_ready, taps_zero, taps_ready = sem("masks_ready"), sem("taps_zero"), sem("taps_ready")
        cond_turned, cond_copied = sem("cond_turned"), sem("cond_copied")
        ctx_done = sem("ctx_done")
        mlp_done, gelu_done = sem("mlp_done"), sem("gelu_done")
        att_step, exp_done, att_turned = sem("att_step"), sem("exp_done"), sem("att_turned")
        attT_copied, spread_ready, aggb_done, attb_done = (sem("attT_copied"), sem("spread_ready"),
                                                           sem("aggb_done"), sem("attb_done"))
        aggb_ready, ctx_ready, attb_ready = sem("aggb_ready"), sem("ctx_ready"), sem("attb_ready")
        wmix_turned, wmix_ready, conv_turned, conv_ready = (sem("wmix_turned"), sem("wmix_ready"),
                                                            sem("conv_turned"), sem("conv_ready"))
        convhi_ready = sem("convhi_ready")
        wmix_copied, lane_copied, lb_copied, b1_copied = (sem("wmix_copied"), sem("lane_copied"),
                                                          sem("lb_copied"), sem("b1_copied"))
        fill_done, fill_hi, fill_lo = sem("fill_done"), sem("fill_hi"), sem("fill_lo")
        prod_done, gsum_done, mixw_done = sem("prod_done"), sem("gsum_done"), sem("mixw_done")
        mix_done, y32_done, yhi_done, ylo_done = sem("mix_done"), sem("y32_done"), sem("yhi_done"), sem("ylo_done")
        up_done, gate0_step, z_ready, zt_done, zT_ready = (sem("up_done"), sem("gate0_step"), sem("z_ready"),
                                                           sem("zt_done"), sem("zT_ready"))
        upgate_done, basegate_done = sem("upgate_done"), sem("basegate_done")
        lb_done, x1_done, x1b_done = sem("lb_done"), sem("x1_done"), sem("x1b_done")
        xqhi_done, xqlo_done, ct_done = sem("xqhi_done"), sem("xqlo_done"), sem("ct_done")
        conv_done, c32_done, chi_done, clo_done = sem("conv_done"), sem("c32_done"), sem("chi_done"), sem("clo_done")
        base_done, gate1_step, d2_ready, e2_ready, hw_done = (sem("base_done"), sem("gate1_step"), sem("d2_ready"),
                                                              sem("e2_ready"), sem("hw_done"))
        ht_done, hthi_done, htlo_done = sem("ht_done"), sem("hthi_done"), sem("htlo_done")
        delta_done, out_done = sem("delta_done"), sem("out_done")

        fills = []
        for q in range(NQ):
            cols = slice(q * NM, (q + 1) * NM)
            fills.append(((in_up[q * 2 // NQ], 16), [wup_raw[:, q, k * P:(k + 1) * P] for k in range(KC)], KC, NM,
                          up_hi[:, :, cols], up_lo[:, :, cols]))
        ga = [ga_raw[:, k * P:(k + 1) * P] for k in range(KC)]
        fills.append(((in_small0, 48), ga, KC, Z0 + E0, up_hi[:, :, H:L0W], up_lo[:, :, H:L0W]))
        LB_FILL = len(fills)
        fills.append(((lb_copied, 1), [lb_rep[:, q].rearrange("m a e r -> m (a e r)")
                                        for q in range(NQ)], NQ, NM, None, None))
        fills.append(((in_gate, 16), [g1_raw[:, q:H:NQ] for q in range(NQ)], NQ, E1,
                      base_hi[:, :, 0, HALF + P:L1W], base_lo[:, :, 0, HALF + P:L1W]))
        for q in range(NQ):
            fills.append(((in_base, 32), [wbase_raw[:, dc, q:H:NQ] for dc in range(KC)], KC, P,
                          base_hi[:, q, :, 0:HALF].rearrange("m j (k d) -> m j k d", k=2),
                          base_lo[:, q, :, 0:HALF].rearrange("m j (k d) -> m j k d", k=2)))
        fills.append(((in_a1, 16), [a1_raw[:, q:H:NQ] for q in range(NQ)], NQ, P,
                      base_hi[:, :, 0, HALF:HALF + P], base_lo[:, :, 0, HALF:HALF + P]))
        fills.append(((b1_copied, 1), [b1m_t[:, q].rearrange("m e r -> m (e r)") for q in range(NQ)], NQ, NM,
                      b1_hi[:].rearrange("p (m q) -> p q m", q=NQ), b1_lo[:].rearrange("p (m q) -> p q m", q=NQ)))
        NF = len(fills)
        NF0 = LB_FILL + 1
        NF1, NF2 = NF0 + 1, NF0 + 1 + NQ
        bank_of = [ps_up[:, 0], ps_up[:, 1], ps_base[:, 0], ps_base[:, 1], ps_ct[:, 0], ps_turn[:, 0],
                   ps_mix[:, 0, SLOTS * C:], ps_base[:, 0], ps_base[:, 1], ps_ct[:, 0], ps_conv[:, 0],
                   ps_base[:, 0], ps_base[:, 1]]
        bank_free = [None, None, None, None, (wmix_ready, 1), None,
                     (y32_done, 1), (fill_lo, 3), (fill_lo, 4), (fill_lo, 5), (ctx_ready, 1),
                     (fill_lo, 8), (fill_lo, 9)]
        assert len(bank_of) == len(bank_free) == NF

        def fill_bank(n, parts=P):
            _, _, cnt, width, hi, _ = fills[n]
            v = bank_of[n][0:parts, 0:cnt * width].rearrange("p (k d) -> p k d", k=cnt)
            if hi is not None and len(hi.shape) == 4:
                v = v.rearrange("p (j k) d -> p j k d", j=2)
            return v

        def once(tile):
            return not isinstance(tile, int) or 0 <= tile < NT

        def after(eng, sem, count):
            if not isinstance(count, int) or count > 0:
                eng.wait_ge(sem, count)

        FIRST, LAST = 4, NT - 2
        STEPS = NT + 2

        def iterate(eng, body):
            for i in range(FIRST):
                body(i, i % 2)
            with eng.Fori(FIRST // 2, LAST // 2) as pair:
                body(pair * 2, 0)
                body(pair * 2 + 1, 1)
            for i in range(LAST, STEPS):
                body(i, i % 2)

        def pair_count(i, par, off):
            return (i + (off - (par + off) % 2)) * 8 + 16

        def position_major(c):
            return c[:].rearrange("m p (b o) -> m b p o", b=SPT)

        block = ctx.enter_context(nc.Block())

        @block.sync
        def _(sp):
            def load_x(t, par):
                sp.dma_start(xt[:, par], x_rows[bass.ds(t * P, P), :]).then_inc(x_in[par], 16)

            def load_base(half):
                k2 = slice(half * KC // 2, (half + 1) * KC // 2)
                sp.dma_start(wbase_raw[:, k2], w_base.rearrange("(k p) h -> p k h", p=P)[:, k2])\
                    .then_inc(in_base, 16)

            sp.dma_start(cond_s[:], cond).then_inc(in_cond, 16)
            sp.dma_start(W0_s[:], W0).then_inc(in_mlp[0], 16)
            sp.dma_start(b0_s[:], b0.rearrange("(p a) -> p a", a=1)).then_inc(in_mlp[0], 16)
            sp.dma_start(W1_s[:], W1).then_inc(in_mlp[1], 16)
            sp.dma_start(b1_s[:], b1.rearrange("(p a) -> p a", a=1)).then_inc(in_mlp[1], 16)
            sp.dma_start(W2_s[:], W2).then_inc(in_mlp[2], 16)
            sp.dma_start(b2_s[:], b2.partition_broadcast(P)).then_inc(in_mlp[2], 16)
            sp.dma_start(biask_s[:], bias_k).then_inc(in_bias, 16)
            sp.dma_start(wmix_s[:], wmix.rearrange("k o i a -> o k (i a)")).then_inc(in_mix, 16)
            for half in range(2):
                q2 = slice(half * NQ // 2, (half + 1) * NQ // 2)
                sp.dma_start(wup_raw[:, q2], w_up.rearrange("(m q) h -> m q h", q=NQ)[:, q2])\
                    .then_inc(in_up[half], 16)
                if half == 0:
                    load_x(0, 0)
            sp.dma_start(wctx_s[:], wctx).then_inc(in_ctx, 16)
            load_base(0)
            sp.wait_ge(aggb_ready, 1)
            sp.dma_start(rows_dram.rearrange("(b o) -> b o", b=B), agg_b[:]).then_inc(rows_out, 16)
            load_base(1)
            sp.wait_ge(rows_out, 16)
            sp.dma_start(rows[:, 0:EARLY], rows_dram[0:EARLY].partition_broadcast(P)).then_inc(rows_in[0], 16)
            load_x(1, 1)
            sp.dma_start(g1_raw[:], w_gate).then_inc(in_gate, 16)
            sp.dma_start(ebias_s[:], ebias.partition_broadcast(P)).then_inc(in_rows, 16)
            for q in range(NQ):
                sp.dma_start(fside_s[q * C:(q + 1) * C], fside.rearrange("(o a) -> o a", a=1))\
                    .then_inc(in_fside, 16)
            sp.dma_start(a1_raw[:], a1.rearrange("e r d -> (e r) d")).then_inc(in_a1, 16)
            sp.dma_start(bbase_s[:], b_base.partition_broadcast(P)).then_inc(in_rows, 16)

            def body(i, par):
                if once(i):
                    sp.wait_ge(x1_done, i + 1)
                    after(sp, xqlo_done, i)
                    for b in range(SPT):
                        sp.dma_start(xq[:, b, 1:1 + NM], x1p[b * C:(b + 1) * C]).then_inc(xq_in, 16)
                    if not isinstance(i, int) or i + 2 < NT:
                        load_x(i + 2, par)
                if isinstance(i, int) and i < REST:
                    part = (B * C - EARLY) // REST
                    cols = slice(EARLY + i * part, B * C if i == REST - 1 else EARLY + (i + 1) * part)
                    sp.dma_start(rows[:, cols], rows_dram[cols].partition_broadcast(P)).then_inc(rows_in[1], 16)
                if once(i - 2):
                    sp.wait_ge(out_done, i - 1)
                    sp.dma_start(out_rows[bass.ds((i - 2) * P, P), :], ot[:, par]).then_inc(stored[par], 16)

            iterate(sp, body)
            for par in range(2):
                sp.wait_ge(stored[par], 16 * (NT // 2))

        @block.gpsimd
        def _(pool):
            pool.memset(ident[:], 0.0).then_inc(ident_zero, 1)
            pool.wait_ge(ident_zero, 1)
            pool.affine_select(out=ident[:], in_=ident[:], compare_op=ALU.not_equal, fill=1.0, base=0,
                               pattern=[[-1, P]], channel_multiplier=1).then_inc(ident_ready, 1)
            pool.dma_start(ga_raw[0:Z0], lora_a.rearrange("e r h -> (e r) h")).then_inc(in_small0, 16)
            pool.dma_start(ga_raw[Z0:Z0 + E0], gate_w).then_inc(in_small0, 16)
            pool.dma_start(lb_raw[:].rearrange("m e q r -> m e (q r)"),
                           lora_b.rearrange("e (m q) r -> m e (q r)", q=NQ)).then_inc(in_small0, 16)
            pool.dma_start(wconv_s[:], wconv.rearrange("o i k -> o (i k)")).then_inc(in_conv, 16)
            pool.iota(iota8[:], [[1, E1]], base=0, channel_multiplier=0,
                      allow_small_or_imprecise_dtypes=True).then_inc(consts_ready, 1)
            pool.iota(iota_e[:], [[1, E0], [0, R0]], base=0, channel_multiplier=0,
                      allow_small_or_imprecise_dtypes=True).then_inc(consts_ready, 1)
            pool.memset(xq[:], 0.0).then_inc(consts_ready, 1)

            def make_prod(t):
                after(pool, gsum_done, t)
                pool.tensor_tensor(prod[:], wmix_t[:], att_b[:, bass.ds(t, 1), :].to_broadcast([P, C, KATT]),
                                   ALU.mult).then_inc(prod_done, 1)

            pool.wait_ge(in_small0, 48)
            for n in range(3):
                cp = pool.tensor_copy(lb_rep[:, :, n], lb_raw[:].rearrange("m e q r -> m q e r"))
            cp.then_inc(lb_copied, 1)
            pool.wait_ge(attb_ready, 1)
            pool.wait_ge(wmix_ready, 1)
            make_prod(0)
            make_prod(1)
            pool.dma_start(b1m_raw[:].rearrange("m e q r -> m e (q r)"),
                           bb1.rearrange("e (m q) r -> m e (q r)", q=NQ)).then_inc(in_b1, 16)
            pool.wait_ge(y32_done, 1)
            pool.wait_ge(yhi_done, 1)
            pool.tensor_tensor(y_lo[:], y32[:], y_hi[:], ALU.subtract).then_inc(ylo_done, 1)
            pool.wait_ge(in_b1, 16)
            pool.tensor_copy(b1m_t[:], b1m_raw[:].rearrange("m e q r -> m q e r")).then_inc(b1_copied, 1)

            def body(i, par):
                if once(i - 1):
                    pool.wait_ge(xqhi_done, i)
                    pool.wait_ge(xq_in, i * XQ)
                    pool.tensor_tensor(xq_lo[:], xq[:], xq_hi[:], ALU.subtract).then_inc(xqlo_done, 1)
                if once(i + 2):
                    make_prod(i + 2)
                if once(i + 1):
                    pool.wait_ge(y32_done, i + 2)
                    pool.wait_ge(yhi_done, i + 2)
                    pool.tensor_tensor(y_lo[:], y32[:], y_hi[:], ALU.subtract).then_inc(ylo_done, 1)
                if isinstance(i, int) and i == 0:
                    pool.wait_ge(in_rows, 32)
                if once(i):
                    pool.wait_ge(x1_done, i + 1)
                    after(pool, out_done, i - 1)
                    pool.tensor_tensor(x1b[:, par].rearrange("p (m q) -> p m q", q=NQ),
                                       x1p[:].rearrange("p q m -> p m q"),
                                       bbase_s[:].rearrange("p (m q) -> p m q", q=NQ),
                                       ALU.add).then_inc(x1b_done, 1)

            iterate(pool, body)

        @block.scalar
        def _(act):
            act.wait_ge(ident_ready, 1)
            act.activation(h1T[:, 0:1], ident[:, 0:1], ACT.Gelu).then_inc(table_loaded, 1)
            act.wait_ge(in_mlp[0], 32)
            act.wait_ge(mlp_done, 1)
            act.wait_ge(table_loaded, 1)
            act.activation(h1T[:], ps_mix[:, 0, 0:P], ACT.Gelu, bias=b0_s[:, 0:1]).then_inc(gelu_done, 1)
            act.wait_ge(in_mlp[1], 32)
            act.wait_ge(mlp_done, 2)
            act.activation(h2T[:], ps_mix[:, 0, 0:P], ACT.Gelu, bias=b1_s[:, 0:1]).then_inc(gelu_done, 1)
            act.activation(ex[:, 0:1], ident[:, 0:1], ACT.Exp).then_inc(table_loaded, 1)

            def high_part(n):
                act.wait_ge(fill_done, n + 1)
                if n == LB_FILL:
                    v = fill_bank(n, 3 * Z0)
                    act.activation(lb_w[0:2 * Z0].rearrange("p (k d) -> p k d", k=NQ), v[0:2 * Z0],
                                   ACT.Copy).then_inc(fill_hi, 1)
                    act.activation(lb_tmp[2 * Z0:].rearrange("p (k d) -> p k d", k=NQ), v[2 * Z0:],
                                   ACT.Copy).then_inc(fill_hi, 1)
                else:
                    act.activation(fills[n][4], fill_bank(n), ACT.Copy).then_inc(fill_hi, 1)

            def y_high(t):
                act.wait_ge(y32_done, t + 1)
                act.activation(y_hi[:], y32[:], ACT.Copy).then_inc(yhi_done, 1)

            act.wait_ge(att_step, 3)
            act.wait_ge(table_loaded, 2)
            act.activation(ex[:], lg[:], ACT.Exp, bias=negm[:, 0:1], accum_out=exsum[:, 0:1]).then_inc(exp_done, 1)
            act.wait_ge(taps_ready, 1)
            for q in range(NQ):
                act.activation(taps_q[:, :, :, q],
                               taps[:, :, :, q:q + SLOTS].rearrange("o g i s -> o s (g i)"), ACT.Copy)\
                    .then_inc(taps_ready, 1)
            for n in range(LB_FILL):
                high_part(n)
            y_high(0)
            high_part(LB_FILL)
            act.wait_ge(conv_turned, 1)
            act.activation(conv_hi[:], ps_mix[:, 0, 0:SLOTS * C].rearrange("p (s o) -> p s o", s=SLOTS),
                           ACT.Copy).then_inc(convhi_ready, 1)
            high_part(NF0)

            def body(i, par):
                if once(i - 2):
                    act.wait_ge(d2_ready, i - 1)
                    act.activation(e2[:], d2[:], ACT.Exp, accum_out=esum[:, 0:1]).then_inc(e2_ready, 1)
                if once(i - 1):
                    if isinstance(i, int) and i == 1:
                        act.wait_ge(consts_ready, 3)
                    act.wait_ge(xq_in, i * XQ)
                    after(act, conv_done, i - 1)
                    act.activation(xq_hi[:], xq[:], ACT.Copy).then_inc(xqhi_done, 1)
                if once(i - 2):
                    act.wait_ge(ht_done, i - 1)
                    act.activation(hT_hi[:], ps_turn[:, 0, 0:P], ACT.Copy).then_inc(hthi_done, 1)
                if isinstance(i, int) and i == 0:
                    high_part(NF1)
                    high_part(NF1 + 1)
                if once(i):
                    act.wait_ge(zt_done, i + 1)
                    act.activation(zT[:], ps_turn[0:3 * Z0, 0, 0:P], ACT.Copy).then_inc(zT_ready, 1)
                if isinstance(i, int) and i == 0:
                    for n in range(NF1 + 2, NF2):
                        high_part(n)
                if once(i - 1):
                    act.wait_ge(ct_done, i)
                    for half in range(2):
                        q2 = slice(half * NQ // 2, (half + 1) * NQ // 2)
                        act.activation(position_major(c_hi)[:, :, q2],
                                       ps_ct[:, 0].rearrange("m (b p o) -> m b p o", b=SPT, p=NQ)[:, :, q2],
                                       ACT.Copy).then_inc(chi_done, 1)
                if once(i + 1):
                    y_high(i + 1)
                if isinstance(i, int) and i == 0:
                    for n in range(NF2, NF):
                        high_part(n)

            iterate(act, body)

        @block.vector
        def _(dve):
            dve.wait_ge(ident_ready, 1)
            dve.tensor_reduce(quad[:], ident[:].rearrange("p (j r) -> p j r", j=SPT), AX_X, ALU.add)\
                .then_inc(masks_ready, 1)
            dve.tensor_reduce(lane4[:], ident[:].rearrange("p (t j) -> p j t", j=SPT), AX_X, ALU.add)\
                .then_inc(masks_ready, 1)
            dve.tensor_reduce(tile_of[:], ident[:].rearrange("p (t j) -> p t j", j=SPT), AX_X, ALU.add)\
                .then_inc(masks_ready, 1)
            dve.tensor_reduce(group_of[:], ident[0:C, 0:C].rearrange("p (g r) -> p g r", g=GROUPS), AX_X, ALU.add)\
                .then_inc(masks_ready, 1)
            dve.memset(gl0[:], LOWEST).then_inc(masks_ready, 1)
            dve.memset(taps[:], 0.0).then_inc(taps_zero, 1)

            def low_part(n):
                dve.wait_ge(fill_hi, n + 1 + (n >= LB_FILL))
                if n == LB_FILL:
                    dve.tensor_tensor(lb_w[2 * Z0:].rearrange("p (k d) -> p k d", k=NQ),
                                      fill_bank(n, 3 * Z0)[2 * Z0:],
                                      lb_tmp[2 * Z0:].rearrange("p (k d) -> p k d", k=NQ),
                                      ALU.subtract).then_inc(fill_lo, 1)
                else:
                    dve.tensor_tensor(fills[n][5], fill_bank(n), fills[n][4], ALU.subtract).then_inc(fill_lo, 1)

            def mix_sums(t):
                dve.wait_ge(prod_done, t + 1)
                dve.tensor_reduce(gsum[:], prod[:], AX_X, ALU.add).then_inc(gsum_done, 1)

            def mix_blocks(t, half):
                if half == 0:
                    dve.wait_ge(gsum_done, t + 1)
                    after(dve, mix_done, t)
                b2 = slice(half * SPT // 2, (half + 1) * SPT // 2)
                dve.tensor_tensor(mix_w[:, b2], gsum[:].unsqueeze(1).to_broadcast([P, SPT // 2, C]),
                                  quad[:, b2].unsqueeze(2).to_broadcast([P, SPT // 2, C]), ALU.mult)\
                    .then_inc(mixw_done, 1)

            def y_sum(t):
                if isinstance(t, int) and t == EARLY // P:
                    dve.wait_ge(rows_in[1], 16 * REST)
                dve.wait_ge(mix_done, t + 1)
                after(dve, ylo_done, t)
                dve.tensor_tensor(y32[:], ps_mix[:, 0].rearrange("p (k r) -> p k r", k=KC),
                                  rows[:, bass.ds(t * P, P)].unsqueeze(1).to_broadcast([P, KC, P]),
                                  ALU.add).then_inc(y32_done, 1)

            dve.wait_ge(cond_turned, 1)
            dve.tensor_copy(condT[:], ps_mix[:, 0, 0:P]).then_inc(cond_copied, 1)
            dve.wait_ge(in_mix, 16)
            dve.tensor_copy(wmix_rep[:], wmix_s[:].unsqueeze(2).to_broadcast([C, KATT, SPT, C]))\
                .then_inc(wmix_copied, 1)
            dve.wait_ge(masks_ready, 5)
            dve.tensor_copy(lane_rep[:], lane4[:].unsqueeze(2).to_broadcast([P, SPT, C])).then_inc(lane_copied, 1)
            dve.wait_ge(in_mlp[2], 32)
            dve.wait_ge(mlp_done, 3)
            dve.tensor_tensor(lg[:], ps_mix[:, 0, 0:KATT], b2_s[:], ALU.add).then_inc(att_step, 1)
            dve.wait_ge(att_step, 1)
            dve.reduce_max(mx[:], lg[:], AX_X).then_inc(att_step, 1)
            dve.wait_ge(att_step, 2)
            dve.tensor_scalar(negm[:], mx[:], -1.0, None, ALU.mult).then_inc(att_step, 1)
            dve.wait_ge(exp_done, 1)
            dve.reciprocal(exrec[:], exsum[:]).then_inc(att_step, 1)
            dve.wait_ge(att_step, 4)
            dve.tensor_scalar(att[:], ex[:], exrec[:, 0:1], None, ALU.mult).then_inc(att_step, 1)
            dve.wait_ge(att_step, 5)
            dve.wait_ge(masks_ready, 5)
            dve.tensor_tensor(att_spread[:], tile_of[:].unsqueeze(2).to_broadcast([P, NT, KATT]),
                              att[:].unsqueeze(1).to_broadcast([P, NT, KATT]), ALU.mult)\
                .then_inc(spread_ready, 1)
            dve.wait_ge(att_turned, 1)
            dve.tensor_copy(attT[:], ps_mix[0:KATT, 0, 0:P]).then_inc(attT_copied, 1)
            dve.wait_ge(in_conv, 16)
            dve.wait_ge(taps_zero, 1)
            dve.tensor_tensor(taps[:, :, :, NQ - 1:NQ - 1 + TAPS],
                              wconv_s[:].rearrange("o (i k) -> o i k", k=TAPS).unsqueeze(1)
                              .to_broadcast([C, GROUPS, GC, TAPS]),
                              group_of[:].unsqueeze(2).unsqueeze(3).to_broadcast([C, GROUPS, GC, TAPS]),
                              ALU.mult).then_inc(taps_ready, 1)
            dve.wait_ge(aggb_done, 1)
            dve.tensor_copy(agg_b[:], ps_mix[:, 0, 0:C]).then_inc(aggb_ready, 1)
            dve.wait_ge(wmix_turned, 1)
            dve.tensor_copy(wmix_t[:], ps_ct[:, 0, 0:KATT * C].rearrange("p (k o) -> p o k", k=KATT))\
                .then_inc(wmix_ready, 1)
            dve.wait_ge(attb_done, 1)
            dve.tensor_copy(att_b[:], ps_conv[:, 0, 0:NT * KATT].rearrange("p (t k) -> p t k", k=KATT))\
                .then_inc(attb_ready, 1)
            mix_sums(0)
            mix_blocks(0, 0)
            mix_blocks(0, 1)
            low_part(0)
            low_part(1)
            dve.wait_ge(wctx_turned, 1)
            dve.tensor_copy(wctxT[:], ps_conv[:, 0, 0:C].unsqueeze(1).to_broadcast([P, NQ, C])).then_inc(wctx_copied, 1)
            low_part(2)
            dve.wait_ge(rows_in[0], 16)
            y_sum(0)
            for n in range(3, NF0):
                low_part(n)
            dve.wait_ge(ctx_done, 1)
            dve.wait_ge(in_fside, 64)
            dve.tensor_scalar(biasT[:], ps_conv[:, 0, 0:B], fside_s[:, 0:1], None, ALU.add).then_inc(ctx_ready, 1)
            dve.wait_ge(convhi_ready, 1)
            dve.wait_ge(fill_hi, NF0 + 2)
            dve.tensor_tensor(conv_lo[:], ps_mix[:, 0, 0:SLOTS * C].rearrange("p (s o) -> p s o", s=SLOTS),
                              conv_hi[:], ALU.subtract).then_inc(conv_ready, 1)
            low_part(NF0)
            dve.wait_ge(in_rows, 32)

            def turned_low(t):
                dve.wait_ge(hthi_done, t + 1)
                dve.tensor_tensor(hT_lo[:], ps_turn[:, 0, 0:P], hT_hi[:], ALU.subtract).then_inc(htlo_done, 1)

            def x1_sum(t, par):
                dve.wait_ge(lb_done, t + 1)
                after(dve, xq_in, t * XQ)
                after(dve, x1b_done, t)
                dve.tensor_tensor(x1p[:].rearrange("p (j q) m -> p j q m", j=2),
                                  ps_up[:, :, 0:HALF].rearrange("p j (q m) -> p j q m", q=2),
                                  xt[:, par].rearrange("p (m j q) -> p j q m", j=2, q=2), ALU.add)\
                    .then_inc(x1_done, 1)

            G1 = 6
            G0 = 4

            def body(i, par):
                if once(i - 2):
                    t = i - 2
                    logits = ps_base[:, 0, HALF + P:L1W]
                    dve.wait_ge(basegate_done, t + 1)
                    if once(i + 1):
                        mix_sums(i + 1)
                    dve.max(m81[:], logits).then_inc(gate1_step, 1)
                    dve.wait_ge(gate1_step, t * G1 + 1)
                    dve.tensor_scalar(d2[:], m81[:, 0:2], m81[:, 0:1], None, ALU.subtract).then_inc(d2_ready, 1)
                    dve.max_index(ix1[:], m81[:], logits).then_inc(gate1_step, 1)
                    dve.wait_ge(gate1_step, t * G1 + 2)
                    dve.tensor_copy(ixf1[:], ix1[:, 0:2]).then_inc(gate1_step, 1)
                    dve.wait_ge(e2_ready, t + 1)
                    dve.reciprocal(erec[:], esum[:]).then_inc(gate1_step, 1)
                    dve.wait_ge(gate1_step, t * G1 + 3)
                    dve.tensor_scalar(r0[:], iota8[:], ixf1[:, 0:1], e2[:, 0:1], ALU.is_equal, ALU.mult)
                    dve.tensor_scalar(r1[:], iota8[:], ixf1[:, 1:2], e2[:, 1:2], ALU.is_equal, ALU.mult)\
                        .then_inc(gate1_step, 1)
                    dve.wait_ge(gate1_step, t * G1 + 5)
                    dve.tensor_tensor(route[:], r0[:], r1[:], ALU.add).then_inc(gate1_step, 1)
                    dve.wait_ge(gate1_step, t * G1 + 6)
                    after(dve, ht_done, t)
                    dve.scalar_tensor_tensor(
                        hw[:], ps_base[:, 0, HALF:HALF + P].rearrange("p (e r) -> p e r", r=R1),
                        erec[:, 0:1], route[:].unsqueeze(2).to_broadcast([P, E1, R1]),
                        ALU.mult, ALU.mult).then_inc(hw_done, 1)
                elif once(i + 1):
                    mix_sums(i + 1)
                if once(i):
                    dve.wait_ge(upgate_done, i + 1)
                    dve.tensor_tensor(gl0[:, 0:E0], ps_up[:, 1, HALF + Z0:HALF + Z0 + E0], ebias_s[:], ALU.add)\
                        .then_inc(gate0_step, 1)
                    dve.wait_ge(gate0_step, i * G0 + 1)
                    if once(i + 1):
                        mix_blocks(i + 1, 0)
                    dve.max(m80[:], gl0[:]).then_inc(gate0_step, 1)
                    dve.wait_ge(gate0_step, i * G0 + 2)
                    if once(i + 1):
                        mix_blocks(i + 1, 1)
                    dve.max_index(ix0[:], m80[:], gl0[:]).then_inc(gate0_step, 1)
                    dve.wait_ge(gate0_step, i * G0 + 3)
                    dve.tensor_copy(ixf0[:], ix0[:, 0:1]).then_inc(gate0_step, 1)
                    dve.wait_ge(gate0_step, i * G0 + 4)
                    dve.scalar_tensor_tensor(zm[:], iota_e[:], ixf0[:, 0:1],
                                             ps_up[:, 1, HALF:HALF + Z0].rearrange("p (e r) -> p e r", r=R0),
                                             ALU.is_equal, ALU.mult).then_inc(z_ready, 1)
                    dve.wait_ge(z_ready, i * 3 + 1)
                    after(dve, zt_done, i)
                    dve.tensor_copy(zc[:, 0:3:2], zm[:].rearrange("p e r -> p (e r)").unsqueeze(1)
                                    .to_broadcast([P, 2, Z0])).then_inc(z_ready, 1)
                    dve.wait_ge(z_ready, i * 3 + 2)
                    dve.tensor_tensor(zc[:, 1], zm[:].rearrange("p e r -> p (e r)"), zc[:, 0], ALU.subtract)\
                        .then_inc(z_ready, 1)
                if once(i - 2):
                    turned_low(i - 2)
                if isinstance(i, int) and i == 0:
                    low_part(NF1)
                    low_part(NF1 + 1)
                final = isinstance(i, int) and i == NT - 1
                if final:
                    x1_sum(i, par)
                if once(i - 1):
                    dve.wait_ge(conv_done, i)
                    after(dve, ct_done, i - 1)
                    for half in range(2):
                        b2 = slice(half * SPT // 2, (half + 1) * SPT // 2)
                        dve.tensor_tensor(c32[:, b2], ps_conv[:, 0].rearrange("p (b m) -> p b m", b=SPT)[:, b2],
                                          biasT[:, bass.ds((i - 1) * SPT + half * (SPT // 2), SPT // 2)].unsqueeze(2)
                                          .to_broadcast([P, SPT // 2, NM]), ALU.add).then_inc(c32_done, 1)
                if once(i - 2):
                    dve.wait_ge(delta_done, i - 1)
                    dve.wait_ge(x1b_done, i - 1)
                    after(dve, stored[par], pair_count(i, par, -4))
                    dve.tensor_tensor(ot[:, par].rearrange("p (j d) -> p j d", j=2), ps_base[:, :, 0:HALF],
                                      x1b[:, par].rearrange("p (j d) -> p j d", j=2), ALU.add)\
                        .then_inc(out_done, 1)
                if once(i) and not final:
                    x1_sum(i, par)
                if once(i - 1):
                    dve.wait_ge(chi_done, i * 2)
                    dve.tensor_tensor(position_major(c_lo),
                                      ps_ct[:, 0].rearrange("m (b p o) -> m b p o", b=SPT, p=NQ),
                                      position_major(c_hi), ALU.subtract).then_inc(clo_done, 1)
                if once(i + 1):
                    y_sum(i + 1)
                if isinstance(i, int) and i == 0:
                    for n in range(NF1 + 2, NF):
                        low_part(n)

            iterate(dve, body)

        @block.tensor
        def _(pe):
            pe.wait_ge(ident_ready, 1)

            def fill(n):
                load, blocks, cnt, width, _, _ = fills[n]
                pe.wait_ge(*load)
                if bank_free[n]:
                    pe.wait_ge(*bank_free[n])
                for k, src in enumerate(blocks):
                    rows_in_, cols = src.shape[0], width
                    outp = 3 * Z0 if n == LB_FILL else P
                    mm = pe.transpose(bank_of[n][0:outp, k * cols:(k + 1) * cols], src,
                                      ident[0:rows_in_, 0:rows_in_])
                mm.then_inc(fill_done, 1)

            pe.wait_ge(in_cond, 16)
            pe.transpose(ps_mix[:, 0, 0:P], cond_s[:], ident[:]).then_inc(cond_turned, 1)
            pe.wait_ge(in_mlp[0], 32)
            pe.wait_ge(cond_copied, 1)
            pe.matmul(ps_mix[:, 0, 0:P], W0_s[:], condT[:], start=True, stop=True).then_inc(mlp_done, 1)
            pe.wait_ge(in_mlp[1], 32)
            pe.wait_ge(gelu_done, 1)
            pe.matmul(ps_mix[:, 0, 0:P], W1_s[:], h1T[:], start=True, stop=True).then_inc(mlp_done, 1)
            pe.wait_ge(in_mlp[2], 32)
            pe.wait_ge(gelu_done, 2)
            pe.matmul(ps_mix[:, 0, 0:KATT], h2T[:], W2_s[:], start=True, stop=True).then_inc(mlp_done, 1)
            pe.wait_ge(wmix_copied, 1)
            for k in range(KATT):
                mm = pe.transpose(ps_ct[:, 0, k * C:(k + 1) * C],
                                  wmix_rep[:, k].rearrange("o b i -> o (b i)"), ident[0:C, 0:C])
            mm.then_inc(wmix_turned, 1)
            pe.wait_ge(att_step, 5)
            pe.transpose(ps_mix[0:KATT, 0, 0:P], att[:], ident[:]).then_inc(att_turned, 1)
            pe.wait_ge(in_bias, 16)
            pe.wait_ge(attT_copied, 1)
            pe.matmul(ps_mix[:, 0, 0:C], attT[:], biask_s[:], start=True, stop=True).then_inc(aggb_done, 1)
            pe.wait_ge(spread_ready, 1)
            pe.wait_ge(lane_copied, 1)
            pe.matmul(ps_conv[:, 0, 0:NT * KATT], lane_rep[:].rearrange("p j o -> p (j o)"),
                      att_spread[:].rearrange("p t k -> p (t k)"), start=True, stop=True)\
                .then_inc(attb_done, 1)

            def turn_hw(t):
                pe.wait_ge(hw_done, t + 1)
                pe.wait_ge(zT_ready, t + 2 if once(t + 1) else NT)
                pe.transpose(ps_turn[:, 0, 0:P], hw[:].rearrange("p e r -> p (e r)"), ident[:])\
                    .then_inc(ht_done, 1)

            def turn_z(t):
                pe.wait_ge(z_ready, t * 3 + 3)
                after(pe, htlo_done, t - 1)
                after(pe, zT_ready, t)
                pe.transpose(ps_turn[0:3 * Z0, 0, 0:P], zc[:].rearrange("p a z -> p (a z)").bitcast(F32),
                             ident[:]).then_inc(zt_done, 1)

            def lora_delta(t):
                pe.wait_ge(zT_ready, t + 1)
                for j in range(2):
                    mm = pe.matmul(ps_up[:, j, 0:HALF], zT[:], lb_w[:, j * HALF:(j + 1) * HALF],
                                   start=False, stop=True, skip_group_check=True)
                mm.then_inc(lb_done, 1)

            def mix(t, par):
                pe.wait_ge(x_in[par], pair_of_x(t, par))
                pe.wait_ge(mixw_done, (t + 1) * 2)
                if isinstance(t, int) and t == 1:
                    pe.wait_ge(conv_ready, 1)
                    pe.wait_ge(fill_lo, NF1)
                for k in range(KC):
                    mm = pe.matmul(ps_mix[:, 0, k * P:(k + 1) * P], xt[:, par, k * P:(k + 1) * P],
                                   mix_w[:].rearrange("p b o -> p (b o)"), start=True, stop=True)
                mm.then_inc(mix_done, 1)

            def pair_of_x(t, par):
                return (t - par) * 8 + 16

            fill(0)
            fill(1)
            pe.wait_ge(in_ctx, 16)
            pe.wait_ge(attb_ready, 1)
            pe.transpose(ps_conv[:, 0, 0:C], wctx_s[:], ident[0:C, 0:C]).then_inc(wctx_turned, 1)
            fill(2)
            pe.wait_ge(aggb_ready, 1)
            mix(0, 0)
            pe.wait_ge(wctx_copied, 1)
            pe.matmul(ps_conv[:, 0, 0:B], wctxT[:].rearrange("c p o -> c (p o)"), condT[:], start=True, stop=True)\
                .then_inc(ctx_done, 1)
            for n in range(3, NF1):
                fill(n)
            pe.wait_ge(taps_ready, 1 + NQ)
            for s in range(SLOTS):
                mm = pe.transpose(ps_mix[:, 0, s * C:(s + 1) * C],
                                  taps_q[:, SLOTS - 1 - s].rearrange("o c q -> o (c q)"), ident[0:C, 0:C])
            mm.then_inc(conv_turned, 1)
            pe.wait_ge(fill_lo, LB_FILL)

            def body(i, par):
                if once(i):
                    pe.wait_ge(yhi_done, i + 1)
                    after(pe, x1_done, i)
                    for j, cols, done in ((1, slice(HALF, L0W), upgate_done), (0, slice(0, HALF), up_done)):
                        into = ps_up[:, j, 0:cols.stop - cols.start]
                        for k in range(KC):
                            for w in (up_hi, up_lo):
                                pe.matmul(into, y_hi[:, k], w[:, k, cols], start=(k == 0 and w is up_hi),
                                          stop=False, skip_group_check=True)
                        if j == 1:
                            pe.wait_ge(ylo_done, i + 1)
                        for k in range(KC):
                            mm = pe.matmul(into, y_lo[:, k], up_hi[:, k, cols], start=False,
                                           stop=(k == KC - 1), skip_group_check=True)
                        mm.then_inc(done, 1)
                if isinstance(i, int) and i == 0:
                    for n in range(NF1, NF2):
                        fill(n)
                    pe.wait_ge(fill_lo, NF0)
                if isinstance(i, int) and i == 1:
                    pe.wait_ge(consts_ready, 3)
                    pe.wait_ge(fill_lo, NF)
                final = isinstance(i, int) and i == NT - 1
                last = isinstance(i, int) and i >= NT
                if once(i - 2) and not last:
                    turn_hw(i - 2)
                if once(i - 1):
                    pe.wait_ge(xqhi_done, i)
                    after(pe, c32_done, (i - 1) * 2)
                    for part, (rhs, weights) in enumerate(((xq_hi, (conv_hi, conv_lo)), (xq_lo, (conv_hi,)))):
                        if part == 1:
                            if last:
                                turn_hw(i - 2)
                            if final:
                                lora_delta(i)
                            pe.wait_ge(xqlo_done, i)
                        for w in weights:
                            for d in (-1, 0, 1):
                                s = NQ - NQ * d
                                mm = pe.matmul(ps_conv[:, 0], w[:, s:s + NQ].rearrange("p s o -> p (s o)"),
                                               rhs[:, :, 1 + d:1 + d + NM], start=(w is conv_hi and part == 0
                                                                                   and d == -1),
                                               stop=(part == 1 and d == 1), skip_group_check=True)
                            if final and part == 0 and w is conv_hi:
                                turn_z(i)
                    mm.then_inc(conv_done, 1)
                elif last:
                    turn_hw(i - 2)
                if once(i) and not final:
                    turn_z(i)
                if once(i - 2):
                    pe.wait_ge(hthi_done, i - 1)
                    for n, (lhs, w) in enumerate(((hT_hi, b1_hi), (hT_hi, b1_lo), (hT_lo, b1_hi))):
                        if n == 2:
                            pe.wait_ge(htlo_done, i - 1)
                        for j in range(2):
                            mm = pe.matmul(ps_base[:, j, 0:HALF], lhs[:], w[:, j * HALF:(j + 1) * HALF],
                                           start=False, stop=(n == 2), skip_group_check=True)
                    mm.then_inc(delta_done, 1)
                if once(i) and not final:
                    lora_delta(i)
                if once(i - 1):
                    after(pe, clo_done, i - 1)
                    for b in range(SPT):
                        if b % (SPT // 2) == 0:
                            pe.wait_ge(c32_done, (i - 1) * 2 + 1 + b // (SPT // 2))
                        mm = pe.transpose(ps_ct[:, 0, b * P:(b + 1) * P], c32[:, b], ident[:])
                    mm.then_inc(ct_done, 1)
                if once(i + 1):
                    mix(i + 1, 1 - par)
                if isinstance(i, int) and i == 0:
                    for n in range(NF2, NF):
                        fill(n)
                if once(i - 1):
                    after(pe, out_done, i - 1)
                    for j, width, done in ((0, L1W, basegate_done), (1, HALF, base_done)):
                        for q in range(NQ):
                            if j == 0 and q % (NQ // 2) == 0:
                                pe.wait_ge(chi_done, (i - 1) * 2 + 1 + q // (NQ // 2))
                            for w in (base_hi, base_lo):
                                pe.matmul(ps_base[:, j, 0:width], c_hi[:, q], w[:, q, j, 0:width],
                                          start=(q == 0 and w is base_hi), stop=False, skip_group_check=True)
                        if j == 0:
                            pe.wait_ge(clo_done, i)
                        for q in range(NQ):
                            mm = pe.matmul(ps_base[:, j, 0:width], c_lo[:, q], base_hi[:, q, j, 0:width],
                                           start=False, stop=(q == NQ - 1), skip_group_check=True)
                        mm.then_inc(done, 1)

            iterate(pe, body)


_INS = ['x', 'cond_128', 'fside_S_0', 'L0_cond_W0', 'L0_cond_b0', 'L0_cond_W1', 'L0_cond_b1', 'L0_cond_W2',
        'L0_cond_b2', 'L0_cond_weight', 'L0_cond_bias_k', 'L0_ffn_W_up', 'L0_ffn_gate_w', 'L0_ffn_expert_bias',
        'L0_ffn_lora_A', 'L0_ffn_lora_B', 'L1_cond_weight', 'L1_cond_c_weight', 'L1_ffn_W_base',
        'L1_ffn_b_base', 'L1_ffn_W_gate', 'L1_ffn_A', 'L1_ffn_B']


def kernel(**inputs):
    import numpy as _np
    import concourse.bacc as _bacc
    from concourse import mybir as _mybir
    from concourse.bass_utils import run_bass_kernel_spmd as _run

    nc = _bacc.Bacc("TRN2", target_bir_lowering=False, num_devices=1)
    arrays, args = {}, []
    for name in _INS:
        a = _np.ascontiguousarray(inputs[name])
        arrays[f"in_{name}"] = a
        args.append(nc.dram_tensor(f"in_{name}", a.shape, _mybir.dt.from_np(a.dtype), kind="ExternalInput").ap())
    out = nc.dram_tensor("out_x", (B, C, H), F32, kind="ExternalOutput")
    adaln_ffn(nc, *args, out.ap())
    return _run(nc, [arrays], core_ids=[0]).results[0]["out_x"]
```
